# Optimizing a Trainium2 kernel written in Bass

```python
import numpy as np
import jax
import jax.numpy as jnp

def _softmax(x, axis=-1):
    return jax.nn.softmax(x, axis=axis)

def _gelu(x):
    return jax.nn.gelu(x, approximate=True)

def _silu(x):
    return jax.nn.silu(x)

def _sigmoid(x):
    return jax.nn.sigmoid(x)

def _layernorm(x, axis=-1, eps=1e-05):
    m = jnp.mean(x, axis=axis, keepdims=True)
    v = jnp.var(x, axis=axis, keepdims=True)
    return (x - m) / jnp.sqrt(v + eps)

def _scatter_add(tgt, idx, src, axis=0):
    return tgt.at[idx].add(src)

def _segment_sum(src, seg, n):
    return jax.ops.segment_sum(src, seg, n)
kernel_name = 'mk_adaln_d2_jaxref_r8_39e927'

def setup_inputs(seed: int=0):
    np.random.seed(seed)
    _w = jnp.asarray

    def _L0_attn_setup():
        import jax, jax.numpy as jnp
        import numpy as np
        H = 8
        D = 64
        E = 128

        def sinusoidal_pe(T, d, dtype=jnp.float32):
            pos = jnp.arange(T, dtype=jnp.float32)[:, None]
            div = jnp.exp(jnp.arange(0, d, 2, dtype=jnp.float32) * (-np.log(10000.0) / d))
            ang = pos * div
            pe = jnp.stack([jnp.sin(ang), jnp.cos(ang)], axis=-1).reshape(T, d)
            return pe.astype(dtype)
        key = jax.random.key(seed)
        k1, k2, k3 = jax.random.split(key, 3)
        B, T = (2, 256)
        x = jax.random.normal(k1, (B, T, E), dtype=jnp.float32)
        Wqkv = jax.random.normal(k2, (3 * H * D, E), dtype=jnp.float32) * (1.0 / np.sqrt(E))
        Wo = jax.random.normal(k3, (E, H * D), dtype=jnp.float32) * (1.0 / np.sqrt(H * D))
        return {'x': x, 'Wqkv': Wqkv, 'Wo': Wo}
    _L0_attn_in = _L0_attn_setup()

    def _L0_ffn_setup():
        import jax, jax.numpy as jnp
        import numpy as np
        DIM = 128
        DEPTH = 2
        HEADS = 8
        DIM_HEAD = 64
        WINDOW = 64
        INNER = HEADS * DIM_HEAD
        HID = int(DIM * 4 * 2 / 3)
        B, N = (2, 1024)
        QK_SCALE = 8.0

        def shift_token(t):
            t1, t2 = jnp.split(t, 2, axis=-1)
            t2 = jnp.pad(t2, ((0, 0), (1, 0), (0, 0)))[:, :-1]
            return jnp.concatenate([t1, t2], axis=-1)

        def l2norm(t):
            return t / jnp.clip(jnp.linalg.norm(t, axis=-1, keepdims=True), 1e-12)

        def rotate_half(x):
            x1, x2 = jnp.split(x, 2, axis=-1)
            return jnp.concatenate([-x2, x1], axis=-1)

        def rotary_xpos(q, k):
            n = q.shape[-2]
            half_idx = jnp.arange(0, DIM_HEAD, 2, dtype=jnp.float32)
            inv_freq = 1.0 / 10000.0 ** (half_idx / DIM_HEAD)
            t = jnp.arange(n, dtype=jnp.float32)
            freqs = t[:, None] * inv_freq[None, :]
            freqs = jnp.concatenate([freqs, freqs], axis=-1)
            base = (half_idx + 0.4 * DIM_HEAD) / (1.4 * DIM_HEAD)
            power = (t - n // 2) / float(WINDOW // 2)
            scale = base[None, :] ** power[:, None]
            scale = jnp.concatenate([scale, scale], axis=-1)
            cos, sin = (jnp.cos(freqs), jnp.sin(freqs))
            q = q * cos * scale + rotate_half(q) * sin * scale
            k = k * cos / scale + rotate_half(k) * sin / scale
            return (q, k)

        def local_attention(q, k, v):
            b, h, n, d = q.shape
            w = n // WINDOW
            bq = q.reshape(b, h, w, WINDOW, d) * QK_SCALE
            bk = k.reshape(b, h, w, WINDOW, d)
            bv = v.reshape(b, h, w, WINDOW, d)

            def look_around(t):
                p = jnp.pad(t, ((0, 0), (0, 0), (1, 0), (0, 0), (0, 0)))
                return jnp.concatenate([p[:, :, :w], p[:, :, 1:]], axis=3)
            bk, bv = (look_around(bk), look_around(bv))
            bt = jnp.arange(n).reshape(w, WINDOW)
            btp = jnp.pad(bt, ((1, 0), (0, 0)), constant_values=-1)
            btk = jnp.concatenate([btp[:w], btp[1:]], axis=1)
            sim = jnp.einsum('bhwid,bhwjd->bhwij', bq, bk)
            i = bt[:, :, None]
            j = btk[:, None, :]
            mask = (i < j) | (i > j + WINDOW) | (j == -1)
            sim = jnp.where(mask, -jnp.finfo(sim.dtype).max, sim)
            attn = jax.nn.softmax(sim, axis=-1)
            out = jnp.einsum('bhwij,bhwjd->bhwid', attn, bv)
            return out.reshape(b, h, n, d)

        def _layer(x, wqkv, qs, ksc, wo, lg, lb, w1, b1, w2, b2):
            b, n, _ = x.shape
            h = shift_token(x)
            qkv = h @ wqkv
            q, k, v = jnp.split(qkv, 3, axis=-1)
            to_heads = lambda t: t.reshape(b, n, HEADS, DIM_HEAD).transpose(0, 2, 1, 3)
            q, k, v = (to_heads(q), to_heads(k), to_heads(v))
            q = l2norm(q) * qs
            k = l2norm(k) * ksc
            q, k = rotary_xpos(q, k)
            o = local_attention(q, k, v)
            o = o.transpose(0, 2, 1, 3).reshape(b, n, INNER)
            x = x + o @ wo
            h = shift_token(x)
            mu = h.mean(-1, keepdims=True)
            var = h.var(-1, keepdims=True)
            h = (h - mu) / jnp.sqrt(var + 1e-05) * lg + lb
            h = h @ w1 + b1
            a, g = jnp.split(h, 2, axis=-1)
            h = a * jax.nn.gelu(g, approximate=False)
            x = x + h @ w2 + b2
            return x
        key = jax.random.key(seed)
        ks = jax.random.split(key, 6)
        return {'x': jax.random.normal(ks[0], (B, N, DIM), jnp.float32), 'wqkv': jax.random.normal(ks[1], (DEPTH, DIM, 3 * INNER), jnp.float32) * 0.02, 'q_scale': jnp.ones((DEPTH, DIM_HEAD), jnp.float32), 'k_scale': jnp.ones((DEPTH, DIM_HEAD), jnp.float32), 'wo': jax.random.normal(ks[2], (DEPTH, INNER, DIM), jnp.float32) * 0.02, 'ln_g': jnp.ones((DEPTH, DIM), jnp.float32), 'ln_b': jnp.zeros((DEPTH, DIM), jnp.float32), 'w1': jax.random.normal(ks[3], (DEPTH, DIM, 2 * HID), jnp.float32) * 0.02, 'b1': jnp.zeros((DEPTH, 2 * HID), jnp.float32), 'w2': jax.random.normal(ks[4], (DEPTH, HID, DIM), jnp.float32) * 0.02, 'b2': jnp.zeros((DEPTH, DIM), jnp.float32)}
    _L0_ffn_in = _L0_ffn_setup()
    _L0_c = _w((lambda *s: np.random.randn(*s).astype(np.float32) * 0.05)(32, 128))
    _L0_wmod = _w((lambda *s: np.random.randn(*s).astype(np.float32) * 0.05)(128, 6 * 128) * 128 ** (-0.5))

    def _L1_attn_setup():
        import jax, jax.numpy as jnp
        import numpy as np
        import math
        D_MODEL = 128
        N_HEADS = 16
        D_HEAD = D_MODEL // N_HEADS
        MAX_SEQ_LEN = 256
        BASE = 10000.0

        def _rope_tables(L):
            pos = jnp.arange(L, dtype=jnp.float32)[:, None]
            freqs = jnp.exp(-math.log(BASE) * jnp.arange(0, D_HEAD, 2, dtype=jnp.float32) / D_HEAD)
            angles = pos * freqs
            return (jnp.sin(angles), jnp.cos(angles))

        def _apply_rope(x, sin, cos):
            s = sin[None, :, None, :]
            c = cos[None, :, None, :]
            x_even, x_odd = (x[..., ::2], x[..., 1::2])
            rot_even = x_even * c - x_odd * s
            rot_odd = x_even * s + x_odd * c
            return jnp.stack([rot_even, rot_odd], axis=-1).reshape(x.shape)
        key = jax.random.key(seed)
        k0, k1, k2, k3, k4 = jax.random.split(key, 5)
        B, L = (2, 256)
        scale = 1.0 / math.sqrt(D_MODEL)
        return {'x': jax.random.normal(k0, (B, L, D_MODEL), dtype=jnp.float32), 'W_q': jax.random.normal(k1, (D_MODEL, D_MODEL), dtype=jnp.float32) * scale, 'W_k': jax.random.normal(k2, (D_MODEL, D_MODEL), dtype=jnp.float32) * scale, 'W_v': jax.random.normal(k3, (D_MODEL, D_MODEL), dtype=jnp.float32) * scale, 'W_o': jax.random.normal(k4, (D_MODEL, D_MODEL), dtype=jnp.float32) * scale}
    _L1_attn_in = _L1_attn_setup()

    def _L1_ffn_setup():
        import jax, jax.numpy as jnp
        import numpy as np
        BLOCK = 16
        _GRID = jnp.array([0.0, 0.5, 1.0, 1.5, 2.0, 3.0, 4.0, 6.0], dtype=jnp.float32)
        _MID = jnp.array([0.25, 0.75, 1.25, 1.75, 2.5, 3.5, 5.0], dtype=jnp.float32)

        def fp4_quant_dequant(x):
            shape = x.shape
            xb = x.reshape(shape[:-1] + (shape[-1] // BLOCK, BLOCK))
            scale = jnp.max(jnp.abs(xb), axis=-1, keepdims=True) / 6.0
            scale = jnp.maximum(scale, jnp.float32(1e-12))
            xn = xb / scale
            idx = jnp.searchsorted(_MID, jnp.abs(xn))
            q = _GRID[idx] * jnp.sign(xn) * scale
            return q.reshape(shape)

        def fp4_linear(x, w):
            xq = fp4_quant_dequant(x)
            wq = fp4_quant_dequant(w)
            return jnp.einsum('bsk,nk->bsn', xq, wq)
        key = jax.random.key(seed)
        k1, k2, k3, k4 = jax.random.split(key, 4)
        H, I = (128, 352)
        x = jax.random.normal(k1, (4, 512, H), dtype=jnp.float32)
        w_gate = jax.random.normal(k2, (I, H), dtype=jnp.float32) * 0.02
        w_up = jax.random.normal(k3, (I, H), dtype=jnp.float32) * 0.02
        w_down = jax.random.normal(k4, (H, I), dtype=jnp.float32) * 0.02
        return {'x': x, 'w_gate': w_gate, 'w_up': w_up, 'w_down': w_down}
    _L1_ffn_in = _L1_ffn_setup()
    _L1_c = _w((lambda *s: np.random.randn(*s).astype(np.float32) * 0.05)(32, 128))
    _L1_wmod = _w((lambda *s: np.random.randn(*s).astype(np.float32) * 0.05)(128, 6 * 128) * 128 ** (-0.5))
    _d = {'L0_attn_x': _L0_attn_in['x'], 'L0_attn_Wqkv': _L0_attn_in['Wqkv'], 'L0_attn_Wo': _L0_attn_in['Wo'], 'L0_ffn_wqkv': _L0_ffn_in['wqkv'], 'L0_ffn_q_scale': _L0_ffn_in['q_scale'], 'L0_ffn_k_scale': _L0_ffn_in['k_scale'], 'L0_ffn_wo': _L0_ffn_in['wo'], 'L0_ffn_ln_g': _L0_ffn_in['ln_g'], 'L0_ffn_ln_b': _L0_ffn_in['ln_b'], 'L0_ffn_w1': _L0_ffn_in['w1'], 'L0_ffn_b1': _L0_ffn_in['b1'], 'L0_ffn_w2': _L0_ffn_in['w2'], 'L0_ffn_b2': _L0_ffn_in['b2'], 'L0_c': _L0_c, 'L0_wmod': _L0_wmod, 'L1_attn_W_q': _L1_attn_in['W_q'], 'L1_attn_W_k': _L1_attn_in['W_k'], 'L1_attn_W_v': _L1_attn_in['W_v'], 'L1_attn_W_o': _L1_attn_in['W_o'], 'L1_ffn_w_gate': _L1_ffn_in['w_gate'], 'L1_ffn_w_up': _L1_ffn_in['w_up'], 'L1_ffn_w_down': _L1_ffn_in['w_down'], 'L1_c': _L1_c, 'L1_wmod': _L1_wmod}
    _x0 = _d['L0_attn_x']
    _d['L0_attn_x'] = jax.random.normal(jax.random.fold_in(jax.random.key(seed), 1), (32, 256, 128), dtype=_x0.dtype)
    del _x0
    return _d

def reference(L0_attn_x, L0_attn_Wqkv, L0_attn_Wo, L0_ffn_wqkv, L0_ffn_q_scale, L0_ffn_k_scale, L0_ffn_wo, L0_ffn_ln_g, L0_ffn_ln_b, L0_ffn_w1, L0_ffn_b1, L0_ffn_w2, L0_ffn_b2, L0_c, L0_wmod, L1_attn_W_q, L1_attn_W_k, L1_attn_W_v, L1_attn_W_o, L1_ffn_w_gate, L1_ffn_w_up, L1_ffn_w_down, L1_c, L1_wmod):

    def _L0_attn_ref(x, Wqkv, Wo):
        import jax, jax.numpy as jnp
        import numpy as np
        H = 8
        D = 64
        E = 128

        def sinusoidal_pe(T, d, dtype=jnp.float32):
            pos = jnp.arange(T, dtype=jnp.float32)[:, None]
            div = jnp.exp(jnp.arange(0, d, 2, dtype=jnp.float32) * (-np.log(10000.0) / d))
            ang = pos * div
            pe = jnp.stack([jnp.sin(ang), jnp.cos(ang)], axis=-1).reshape(T, d)
            return pe.astype(dtype)
        B, T, _ = x.shape
        qkv = jnp.einsum('bte,fe->btf', x, Wqkv)
        qkv = qkv.reshape(B, T, H, 3 * D)
        q, k, v = jnp.split(qkv, 3, axis=-1)
        q = q.transpose(0, 2, 1, 3)
        k = k.transpose(0, 2, 1, 3)
        v = v.transpose(0, 2, 1, 3)
        pe = sinusoidal_pe(T, D, q.dtype)
        q = q + pe[None, None]
        k = k + pe[None, None]
        causal = jnp.tril(jnp.ones((T, T), dtype=bool))
        scores = jnp.einsum('bhtd,bhsd->bhts', q, k) / jnp.sqrt(jnp.asarray(D, q.dtype))
        scores = jnp.where(causal[None, None], scores, jnp.asarray(-jnp.inf, q.dtype))
        probs = jax.nn.softmax(scores, axis=-1)
        attn = jnp.einsum('bhts,bhsd->bhtd', probs, v)
        out = attn.transpose(0, 2, 1, 3).reshape(B, T, H * D)
        out = jnp.einsum('btf,ef->bte', out, Wo)
        return out

    def _L0_ffn_ref(x, wqkv, q_scale, k_scale, wo, ln_g, ln_b, w1, b1, w2, b2):
        import jax, jax.numpy as jnp
        import numpy as np
        DIM = 128
        DEPTH = 2
        HEADS = 8
        DIM_HEAD = 64
        WINDOW = 64
        INNER = HEADS * DIM_HEAD
        HID = int(DIM * 4 * 2 / 3)
        B, N = (2, 1024)
        QK_SCALE = 8.0

        def shift_token(t):
            t1, t2 = jnp.split(t, 2, axis=-1)
            t2 = jnp.pad(t2, ((0, 0), (1, 0), (0, 0)))[:, :-1]
            return jnp.concatenate([t1, t2], axis=-1)

        def l2norm(t):
            return t / jnp.clip(jnp.linalg.norm(t, axis=-1, keepdims=True), 1e-12)

        def rotate_half(x):
            x1, x2 = jnp.split(x, 2, axis=-1)
            return jnp.concatenate([-x2, x1], axis=-1)

        def rotary_xpos(q, k):
            n = q.shape[-2]
            half_idx = jnp.arange(0, DIM_HEAD, 2, dtype=jnp.float32)
            inv_freq = 1.0 / 10000.0 ** (half_idx / DIM_HEAD)
            t = jnp.arange(n, dtype=jnp.float32)
            freqs = t[:, None] * inv_freq[None, :]
            freqs = jnp.concatenate([freqs, freqs], axis=-1)
            base = (half_idx + 0.4 * DIM_HEAD) / (1.4 * DIM_HEAD)
            power = (t - n // 2) / float(WINDOW // 2)
            scale = base[None, :] ** power[:, None]
            scale = jnp.concatenate([scale, scale], axis=-1)
            cos, sin = (jnp.cos(freqs), jnp.sin(freqs))
            q = q * cos * scale + rotate_half(q) * sin * scale
            k = k * cos / scale + rotate_half(k) * sin / scale
            return (q, k)

        def local_attention(q, k, v):
            b, h, n, d = q.shape
            w = n // WINDOW
            bq = q.reshape(b, h, w, WINDOW, d) * QK_SCALE
            bk = k.reshape(b, h, w, WINDOW, d)
            bv = v.reshape(b, h, w, WINDOW, d)

            def look_around(t):
                p = jnp.pad(t, ((0, 0), (0, 0), (1, 0), (0, 0), (0, 0)))
                return jnp.concatenate([p[:, :, :w], p[:, :, 1:]], axis=3)
            bk, bv = (look_around(bk), look_around(bv))
            bt = jnp.arange(n).reshape(w, WINDOW)
            btp = jnp.pad(bt, ((1, 0), (0, 0)), constant_values=-1)
            btk = jnp.concatenate([btp[:w], btp[1:]], axis=1)
            sim = jnp.einsum('bhwid,bhwjd->bhwij', bq, bk)
            i = bt[:, :, None]
            j = btk[:, None, :]
            mask = (i < j) | (i > j + WINDOW) | (j == -1)
            sim = jnp.where(mask, -jnp.finfo(sim.dtype).max, sim)
            attn = jax.nn.softmax(sim, axis=-1)
            out = jnp.einsum('bhwij,bhwjd->bhwid', attn, bv)
            return out.reshape(b, h, n, d)

        def _layer(x, wqkv, qs, ksc, wo, lg, lb, w1, b1, w2, b2):
            b, n, _ = x.shape
            h = shift_token(x)
            qkv = h @ wqkv
            q, k, v = jnp.split(qkv, 3, axis=-1)
            to_heads = lambda t: t.reshape(b, n, HEADS, DIM_HEAD).transpose(0, 2, 1, 3)
            q, k, v = (to_heads(q), to_heads(k), to_heads(v))
            q = l2norm(q) * qs
            k = l2norm(k) * ksc
            q, k = rotary_xpos(q, k)
            o = local_attention(q, k, v)
            o = o.transpose(0, 2, 1, 3).reshape(b, n, INNER)
            x = x + o @ wo
            h = shift_token(x)
            mu = h.mean(-1, keepdims=True)
            var = h.var(-1, keepdims=True)
            h = (h - mu) / jnp.sqrt(var + 1e-05) * lg + lb
            h = h @ w1 + b1
            a, g = jnp.split(h, 2, axis=-1)
            h = a * jax.nn.gelu(g, approximate=False)
            x = x + h @ w2 + b2
            return x
        for l in range(DEPTH):
            x = _layer(x, wqkv[l], q_scale[l], k_scale[l], wo[l], ln_g[l], ln_b[l], w1[l], b1[l], w2[l], b2[l])
        return x

    def _L1_attn_ref(x, W_q, W_k, W_v, W_o):
        import jax, jax.numpy as jnp
        import numpy as np
        import math
        D_MODEL = 128
        N_HEADS = 16
        D_HEAD = D_MODEL // N_HEADS
        MAX_SEQ_LEN = 256
        BASE = 10000.0

        def _rope_tables(L):
            pos = jnp.arange(L, dtype=jnp.float32)[:, None]
            freqs = jnp.exp(-math.log(BASE) * jnp.arange(0, D_HEAD, 2, dtype=jnp.float32) / D_HEAD)
            angles = pos * freqs
            return (jnp.sin(angles), jnp.cos(angles))

        def _apply_rope(x, sin, cos):
            s = sin[None, :, None, :]
            c = cos[None, :, None, :]
            x_even, x_odd = (x[..., ::2], x[..., 1::2])
            rot_even = x_even * c - x_odd * s
            rot_odd = x_even * s + x_odd * c
            return jnp.stack([rot_even, rot_odd], axis=-1).reshape(x.shape)
        B, L, _ = x.shape
        sin, cos = _rope_tables(L)
        q = (x @ W_q.T).reshape(B, L, N_HEADS, D_HEAD)
        k = (x @ W_k.T).reshape(B, L, N_HEADS, D_HEAD)
        v = (x @ W_v.T).reshape(B, L, N_HEADS, D_HEAD)
        q = _apply_rope(q, sin, cos)
        k = _apply_rope(k, sin, cos)
        scores = jnp.einsum('blhd,bshd->bhls', q, k) / math.sqrt(D_HEAD)
        weights = jax.nn.softmax(scores, axis=-1)
        out = jnp.einsum('bhls,bshd->blhd', weights, v).reshape(B, L, D_MODEL)
        return out @ W_o.T

    def _L1_ffn_ref(x, w_gate, w_up, w_down):
        import jax, jax.numpy as jnp
        import numpy as np
        BLOCK = 16
        _GRID = jnp.array([0.0, 0.5, 1.0, 1.5, 2.0, 3.0, 4.0, 6.0], dtype=jnp.float32)
        _MID = jnp.array([0.25, 0.75, 1.25, 1.75, 2.5, 3.5, 5.0], dtype=jnp.float32)

        def fp4_quant_dequant(x):
            shape = x.shape
            xb = x.reshape(shape[:-1] + (shape[-1] // BLOCK, BLOCK))
            scale = jnp.max(jnp.abs(xb), axis=-1, keepdims=True) / 6.0
            scale = jnp.maximum(scale, jnp.float32(1e-12))
            xn = xb / scale
            idx = jnp.searchsorted(_MID, jnp.abs(xn))
            q = _GRID[idx] * jnp.sign(xn) * scale
            return q.reshape(shape)

        def fp4_linear(x, w):
            xq = fp4_quant_dequant(x)
            wq = fp4_quant_dequant(w)
            return jnp.einsum('bsk,nk->bsn', xq, wq)
        gate = fp4_linear(x, w_gate)
        y = fp4_linear(x, w_up)
        h = jax.nn.silu(gate) * y
        return fp4_linear(h, w_down)
    x = L0_attn_x
    mod = (_silu(L0_c) @ L0_wmod).reshape(L0_c.shape[0], 6, 1, -1)
    sa, ca, ga, sb, cb, gb = (mod[:, 0], mod[:, 1], mod[:, 2], mod[:, 3], mod[:, 4], mod[:, 5])
    ga = (2 * (ga >= 0) - 1) * jnp.maximum(jnp.abs(ga), 0.25)
    gb = (2 * (gb >= 0) - 1) * jnp.maximum(jnp.abs(gb), 0.25)
    h = _layernorm(x, axis=-1) * (1 + ca) + sa
    x = x + ga * _L0_attn_ref(h, L0_attn_Wqkv, L0_attn_Wo)
    h = _layernorm(x, axis=-1) * (1 + cb) + sb
    x = x + gb * _L0_ffn_ref(h, L0_ffn_wqkv, L0_ffn_q_scale, L0_ffn_k_scale, L0_ffn_wo, L0_ffn_ln_g, L0_ffn_ln_b, L0_ffn_w1, L0_ffn_b1, L0_ffn_w2, L0_ffn_b2)
    mod = (_silu(L1_c) @ L1_wmod).reshape(L1_c.shape[0], 6, 1, -1)
    sa, ca, ga, sb, cb, gb = (mod[:, 0], mod[:, 1], mod[:, 2], mod[:, 3], mod[:, 4], mod[:, 5])
    ga = (2 * (ga >= 0) - 1) * jnp.maximum(jnp.abs(ga), 0.25)
    gb = (2 * (gb >= 0) - 1) * jnp.maximum(jnp.abs(gb), 0.25)
    h = _layernorm(x, axis=-1) * (1 + ca) + sa
    x = x + ga * _L1_attn_ref(h, L1_attn_W_q, L1_attn_W_k, L1_attn_W_v, L1_attn_W_o)
    h = _layernorm(x, axis=-1) * (1 + cb) + sb
    x = x + gb * _L1_ffn_ref(h, L1_ffn_w_gate, L1_ffn_w_up, L1_ffn_w_down)
    return x

_drawn_inputs = setup_inputs


def setup_inputs(seed=0):
    import zlib

    import numpy as np

    out = dict(_drawn_inputs(seed))
    spreads = {'L0_ffn_q_scale': (1.0, 0.6),
     'L0_ffn_k_scale': (1.0, 0.6),
     'L0_ffn_ln_g': (1.0, 0.6),
     'L0_ffn_ln_b': (0.0, 0.8),
     'L0_ffn_b1': (0.0, 0.8),
     'L0_ffn_b2': (0.0, 0.481)}
    factors = {'L0_ffn_wqkv': 6.836,
     'L0_ffn_wo': 6.866,
     'L0_ffn_w1': 8.0,
     'L0_ffn_w2': 8.0,
     'L1_ffn_w_gate': 8.0,
     'L1_ffn_w_up': 8.0,
     'L1_ffn_w_down': 8.0,
     'L1_attn_W_q': 8.0,
     'L1_attn_W_k': 8.0,
     'L1_attn_W_v': 3.826,
     'L1_attn_W_o': 3.791}
    for name, (base, spread) in spreads.items():
        noise = np.random.default_rng([zlib.crc32(name.encode()), seed]).standard_normal(out[name].shape)
        drawn = base * np.exp(spread * noise) if base else spread * noise
        out[name] = jnp.asarray(drawn.astype(out[name].dtype))
    for name, factor in factors.items():
        out[name] = (out[name] * factor).astype(out[name].dtype)
    return out
```

```python
import math
from contextlib import ExitStack

import concourse.bass as bass
from concourse import mybir

ALU = mybir.AluOpType
ACT = mybir.ActivationFunctionType
AX_X = mybir.AxisListType.X
F32 = mybir.dt.float32
BF16 = mybir.dt.bfloat16
U32 = mybir.dt.uint32

P = 128
T = 256
NT = T // P
LANES = 2
HEADS, DH = 8, 64
INNER = HEADS * DH
CHEADS, CDH = 16, 8
CHUNKS = INNER // P
DEPTH = 2
HID = 341
HID_ROWS = [128, 128, HID - 256]
FF = 352
FF_ROWS = [128, 128, FF - 256]
BLOCK = 16
WINDOW = 64
N_LN = 6
N_HEADS = 3 * HEADS + CHEADS
N_MOD = 6
QSTEPS = 15
EXP_LN_SET = 6
SS_SCALE = 2.0 ** 17


def bank_uses():
    uses = [("x", 0)]

    def norm(k):
        uses.extend([(f"mean{k}", 2), (f"var{k}", 3)])

    def core(first, heads, group):
        for h in range(heads + 2):
            if h < heads:
                uses.append((f"S{first + h}", (first + h) % 2))
            if 1 <= h <= heads:
                uses.append((f"P{first + h - 1}", 2))
            if h >= 2 and (h - 2) % group == 0:
                uses.append((f"O{first + h - 2}", 3))

    norm(0)
    uses += [("A.q0", 0), ("A.q1", 1), ("A.k0", 2), ("A.k1", 3), ("A.v0", 0), ("A.v1", 1)]
    core(0, HEADS, 2)
    uses += [("A.oT0", 0), ("A.oT1", 1), ("A.out", 2)]
    norm(1)
    for l in range(DEPTH):
        uses += [(f"B{l}.{n}", b) for n, b in (("q0", 0), ("q1", 1), ("k0", 2), ("k1", 3), ("v0", 0), ("v1", 1),
                                               ("qT0", 2), ("qT1", 3), ("kT0", 0), ("kT1", 1))]
        core(HEADS * (1 + l), HEADS, 2)
        uses += [(f"B{l}.oT0", 0), (f"B{l}.oT1", 1), (f"B{l}.out", 2)]
        norm(2 + l)
        uses += [(f"B{l}.g01", 0), (f"B{l}.g2", 1), (f"B{l}.a01", 2), (f"B{l}.a2", 3), (f"B{l}.y", 0)]
    norm(4)
    uses += [("C.q", 0), ("C.k", 1), ("C.v", 2)]
    core(3 * HEADS, CHEADS, CHEADS)
    uses += [("C.oT", 0), ("C.out", 1)]
    norm(5)
    uses += [("D.h", 0), ("D.xT", 1), ("D.g0", 2), ("D.g1", 3), ("D.u0", 0), ("D.u1", 1),
             ("D.hT0", 2), ("D.hT1", 3), ("D.out", 0), ("out", 1)]
    return uses


def count_uses(uses):
    total, place = [0] * 4, {}
    for name, b in uses:
        assert name not in place
        place[name] = (b, total[b])
        total[b] += 1
    return place, total


def adaln_program(nc, a, out, n_batch):
    ctx = ExitStack()
    with ctx:
        build(nc, ctx, a, out, n_batch)


def build(nc, ctx, a, out, n_batch):
    def sb(name, shape, dt=F32):
        return ctx.enter_context(nc.sbuf_tensor(name, shape, dt))

    def per_lane(name, shape, dt=F32):
        return [sb(f"{name}_{L}", shape, dt) for L in range(LANES)]

    def sem(name):
        return ctx.enter_context(nc.semaphore(name))

    def lane_sem(name):
        return [sem(f"{name}_{L}") for L in range(LANES)]

    place, per_batch = count_uses(bank_uses())
    loops = n_batch // LANES

    ident = sb("ident", [P, P])
    ident_bf = sb("ident_bf", [P, P], BF16)
    mean_w = sb("mean_w", [P, P])
    mask_bf = sb("mask_bf", [P, 2, 3 * P], BF16)
    pe_q = sb("pe_q", [P, T])
    pe_k = sb("pe_k", [P, T])
    wqkv_a = sb("wqkv_a", [P, 3 * INNER])
    wo_a = sb("wo_a", [P, CHUNKS, P])
    wqkv_b = sb("wqkv_b", [P, DEPTH, 3 * INNER])
    wo_b = sb("wo_b", [P, DEPTH, CHUNKS, P])
    w1 = sb("w1", [P, DEPTH, 2 * HID])
    w2 = sb("w2", [P, DEPTH, 3, P])
    xpos = sb("xpos", [P, DEPTH, NT, 4, DH])
    head_scale = sb("head_scale", [P, DEPTH, 4, DH])
    ln_g = sb("ln_g", [P, DEPTH])
    ln_b = sb("ln_b", [P, DEPTH])
    b1a = sb("b1a", [P, DEPTH, 3])
    b1g = sb("b1g", [P, DEPTH, 3])
    b2 = sb("b2", [P, DEPTH])
    w_c = sb("w_c", [P, 6, P])
    rope_c = sb("rope_c", [P, 4, T])
    head_rows = sb("head_rows", [P, CHEADS])
    wg_q = sb("wg_q", [P, FF])
    wu_q = sb("wu_q", [P, FF])
    wd_q = sb("wd_q", [P, 3, P])
    mod_t = sb("mod_t", [P, n_batch, 2 * N_MOD])
    c_t = sb("c_t", [P, 2, n_batch])
    eps_col = sb("eps_col", [P, 1])
    ss_bias = sb("ss_bias", [P, 1])

    x_in = per_lane("x_in", [P, NT, P])
    x_out = per_lane("x_out", [P, NT, P])
    mod = per_lane("mod", [P, 2 * N_MOD])
    xT = per_lane("xT", [P, T])
    yT = per_lane("yT", [P, T])
    shifted = per_lane("shifted", [P, T + 1])
    centred = per_lane("centred", [P, T])
    square = per_lane("square", [P, T])
    rstd = per_lane("rstd", [P, T])
    hT = per_lane("hT", [P, T])
    qT = per_lane("qT", [P, CHUNKS, T])
    kT = per_lane("kT", [P, CHUNKS, T])
    v_ab = per_lane("v_ab", [P, NT, HEADS, DH + 1])
    v_c = per_lane("v_c", [P, NT, CHEADS, CDH + 1])
    negmax = per_lane("negmax", [P, 2, NT])
    probs = per_lane("probs", [P, 2, 2 * T])
    probsT = per_lane("probsT", [P, 2, 2 * T])
    rz = per_lane("rz", [P, 2 * CHEADS])
    o = per_lane("o", [P, NT, INNER])
    oT = per_lane("oT", [P, CHUNKS, T])
    qk_cos = per_lane("qk_cos", [P, 4, INNER])
    qk_sin = per_lane("qk_sin", [P, 2, INNER])
    qk_ss = per_lane("qk_ss", [P, 4, HEADS])
    qk_rn = per_lane("qk_rn", [P, 4, HEADS])
    k_heads = per_lane("k_heads", [P, CHEADS, T])
    q_c = per_lane("q_c", [P, 2, T])
    k_c = per_lane("k_c", [P, 2, T])
    ff_h = per_lane("ff_h", [P, NT * FF])
    ff_s = per_lane("ff_s", [P, 2, NT * FF // BLOCK])

    def beside_heads(first, n):
        return [k_heads[L][:].rearrange("p a n -> p (a n)")[:, first:first + n] for L in range(LANES)]

    def thirds(views):
        return [t.rearrange("p (c t) -> p c t", c=3) for t in views]

    gelu = thirds(beside_heads(0, 3 * T))
    hid = thirds(beside_heads(3 * T, 3 * T))
    qk_sq = [t.rearrange("p (a n) -> p a n", a=2) for t in beside_heads(6 * T, 2 * INNER)]
    ff_n, ff_a, ff_c, ff_d = (beside_heads(n * NT * FF, NT * FF) for n in range(4))
    hT_q = thirds(beside_heads(4 * NT * FF, 3 * T))

    bank = [[ctx.enter_context(nc.psum_tensor(f"bank{L}_{b}", [P, 512], F32)) for b in range(4)]
            for L in range(LANES)]

    loaded = sem("loaded")
    ready_dve = sem("ready_dve")
    ready_act = sem("ready_act")
    ready_pool = sem("ready_pool")
    ready_pe = sem("ready_pe")
    x_loaded = lane_sem("x_loaded")
    x_stored = lane_sem("x_stored")
    out_ready = lane_sem("out_ready")
    mod_ready = lane_sem("mod_ready")
    filled = [[sem(f"filled{b}_{L}") for b in range(4)] for L in range(LANES)]
    taken = [[sem(f"taken{b}_{L}") for b in range(4)] for L in range(LANES)]
    s_centred = lane_sem("s_centred")
    s_square = lane_sem("s_square")
    s_logvar = lane_sem("s_logvar")
    s_rstd = lane_sem("s_rstd")
    s_rstd2 = lane_sem("s_rstd2")
    s_newton = lane_sem("s_newton")
    s_normed = lane_sem("s_normed")
    s_h = lane_sem("s_h")
    s_x = lane_sem("s_x")
    s_y = lane_sem("s_y")
    s_shift = lane_sem("s_shift")
    s_max = lane_sem("s_max")
    s_rz = lane_sem("s_rz")
    s_o = lane_sem("s_o")
    s_qksq = lane_sem("s_qksq")
    s_qkcs = lane_sem("s_qkcs")
    s_ss = lane_sem("s_ss")
    s_ssclamp = lane_sem("s_ssclamp")
    s_logss = lane_sem("s_logss")
    s_rnorm0 = lane_sem("s_rnorm0")
    s_rnorm_step = lane_sem("s_rnorm_step")
    s_rnorm = lane_sem("s_rnorm")
    s_rotsum = lane_sem("s_rotsum")
    s_rot = lane_sem("s_rot")
    s_gelu = lane_sem("s_gelu")
    s_hid = lane_sem("s_hid")
    s_ropec = lane_sem("s_ropec")
    s_qkc = lane_sem("s_qkc")
    s_kheads = lane_sem("s_kheads")
    s_silu = lane_sem("s_silu")
    s_ffh = lane_sem("s_ffh")
    s_q4 = lane_sem("s_q4")

    def is_filled(L, i, name):
        b, n = place[name]
        return filled[L][b], i * per_batch[b] + n + 1

    def is_taken(L, i, name):
        b, n = place[name]
        return taken[L][b], i * per_batch[b] + n + 2

    def is_free(L, i, name):
        b, n = place[name]
        return taken[L][b], i * per_batch[b] + n + 1

    def ps(L, name):
        return bank[L][place[name][0]]

    def sem_filled(L, name):
        return filled[L][place[name][0]]

    def sem_taken(L, name):
        return taken[L][place[name][0]]

    CORES = [("A", 0, HEADS), ("B0", HEADS, HEADS), ("B1", 2 * HEADS, HEADS), ("C", 3 * HEADS, CHEADS)]
    N_MAX = 2 * 3 * HEADS + CHEADS
    N_NORMS = 3 * HEADS // 2 + 1

    def maxima(g):
        return 2 * min(g + 1, 3 * HEADS) + max(0, g + 1 - 3 * HEADS)

    def fp4(dve, src, dst, L, step_sem, base, n, rows=P):
        v = nc.vector
        nb = n // BLOCK

        def blocks(t):
            return t.rearrange("p (b e) -> p b e", e=BLOCK)

        xn, ab, hi, lo = (t[L][0:rows, 0:n] for t in (ff_n, ff_a, ff_c, ff_d))
        scale, inv = ff_s[L][0:rows, 0, 0:nb], ff_s[L][0:rows, 1, 0:nb]

        def over_block(s):
            return s.unsqueeze(2).broadcast_to([rows, nb, BLOCK])

        v.tensor_reduce(inv, blocks(src), AX_X, ALU.max, apply_absolute_value=True).then_inc(step_sem, 1)
        dve.wait_ge(step_sem, base + 1)
        v.tensor_scalar(scale, inv, 1.0 / 6.0, 1e-12, ALU.mult, ALU.max).then_inc(step_sem, 1)
        dve.wait_ge(step_sem, base + 2)
        v.reciprocal(inv, scale).then_inc(step_sem, 1)
        dve.wait_ge(step_sem, base + 3)
        v.tensor_tensor(blocks(xn), blocks(src), over_block(inv), ALU.mult).then_inc(step_sem, 1)
        dve.wait_ge(step_sem, base + 4)
        v.tensor_scalar(ab.bitcast(U32), xn.bitcast(U32), 0x7FFFFFFF, None, ALU.bitwise_and).then_inc(step_sem, 1)
        dve.wait_ge(step_sem, base + 5)
        v.tensor_scalar(hi, ab, 5.0, 2.0, ALU.is_gt, ALU.mult).then_inc(step_sem, 1)
        v.tensor_scalar(lo, ab, 1.75, None, ALU.is_gt).then_inc(step_sem, 1)
        dve.wait_ge(step_sem, base + 6)
        v.scalar_tensor_tensor(hi, ab, 3.5, hi, ALU.is_gt, ALU.add).then_inc(step_sem, 1)
        dve.wait_ge(step_sem, base + 7)
        v.scalar_tensor_tensor(lo, ab, 1.25, lo, ALU.is_gt, ALU.add).then_inc(step_sem, 1)
        dve.wait_ge(step_sem, base + 8)
        v.scalar_tensor_tensor(hi, ab, 2.5, hi, ALU.is_gt, ALU.add).then_inc(step_sem, 1)
        dve.wait_ge(step_sem, base + 9)
        v.scalar_tensor_tensor(lo, ab, 0.75, lo, ALU.is_gt, ALU.add).then_inc(step_sem, 1)
        dve.wait_ge(step_sem, base + 11)
        v.scalar_tensor_tensor(lo, ab, 0.25, lo, ALU.is_gt, ALU.add).then_inc(step_sem, 1)
        dve.wait_ge(step_sem, base + 12)
        v.scalar_tensor_tensor(hi, lo, 0.5, hi, ALU.mult, ALU.add).then_inc(step_sem, 1)
        dve.wait_ge(step_sem, base + 13)
        v.scalar_tensor_tensor(hi.bitcast(U32), xn.bitcast(U32), 0x80000000, hi.bitcast(U32),
                               ALU.bitwise_and, ALU.bitwise_or).then_inc(step_sem, 1)
        dve.wait_ge(step_sem, base + 14)
        v.tensor_tensor(blocks(dst), blocks(hi), over_block(scale), ALU.mult).then_inc(step_sem, 1)

    def setup_loads():
        yield ident[:], a["c_ident"]
        yield masks, a["c_masks"].rearrange("m p n -> p m n")
        yield pe_q[:], a["c_pe_q"]
        yield pe_k[:], a["c_pe_k"]
        yield wqkv_a[:], a["wqkv_a"]
        yield wo_a[:], a["wo_a"].rearrange("(c p) e -> p c e", p=P)
        yield wqkv_b[:], a["wqkv_b"].rearrange("l p n -> p l n")
        yield wo_b[:], a["wo_b"].rearrange("l (c p) e -> p l c e", p=P)
        yield w1[:], a["w1"].rearrange("l p n -> p l n")
        for l in range(DEPTH):
            yield w2[:, l, 0:2, :], a["w2"][l, 0:2 * P, :].rearrange("(c p) e -> p c e", p=P)
            yield w2[0:HID_ROWS[2], l, 2, :], a["w2"][l, 2 * P:HID, :]
            half = DH // 2
            for n, name in ((0, "q_scale"), (2, "k_scale")):
                row = a[name][l:l + 1, :]
                yield head_scale[:, l, n, :], row.broadcast_to([P, DH])
                yield head_scale[:, l, n + 1, 0:half], row[:, half:DH].broadcast_to([P, half])
                yield head_scale[:, l, n + 1, half:DH], row[:, 0:half].broadcast_to([P, half])
            for t, name in ((ln_g, "ln_g"), (ln_b, "ln_b"), (b2, "b2")):
                yield t[:, l:l + 1], a[name][l, :].rearrange("(p o) -> p o", o=1)
            for t, first in ((b1a, 0), (b1g, HID)):
                for c, rows in enumerate(HID_ROWS):
                    at = first + c * P
                    yield t[0:rows, l, c:c + 1], a["b1"][l, at:at + rows].rearrange("(p o) -> p o", o=1)
            yield xpos[:, l], a["c_xpos"].rearrange("t p n d -> p t n d")
        yield w_c[:], a["w_c"].rearrange("n p e -> p n e")
        yield rope_c[:], a["c_rope"].rearrange("n p t -> p n t")
        yield head_rows[:], a["c_head_rows"]
        yield c_t[:], a["c_t"].rearrange("l p b -> p l b")
        for l in range(2):
            yield w_mod[l], a["wmod"][l]
        for flat, name in ((w_nat[0], "w_gate"), (w_nat[1], "w_up")):
            yield flat[:, 0:2 * P].rearrange("p (c k) -> p c k", c=2), a[name][0:2 * P, :].rearrange("(c p) k -> p c k", p=P)
            yield flat[0:FF_ROWS[2], 2 * P:3 * P], a[name][2 * P:FF, :]
        yield ff_h[1][:, 0:FF], a["w_down"]

    masks = o[0][:].rearrange("p t n -> p (t n)")[:, 0:2 * 3 * P].rearrange("p (m n) -> p m n", m=2)
    qk_flat = [qk_cos[l][:].rearrange("p a n -> p (a n)") for l in range(2)]
    w_mod = [t[:, 0:N_MOD * P] for t in qk_flat]
    w_nat = [t[:, N_MOD * P:(N_MOD + 3) * P] for t in qk_flat]
    n_loads = len(list(setup_loads()))
    ALL_LOADED = 16 * n_loads

    block = ctx.enter_context(nc.Block())

    @block.sync
    def _(sp):
        sp.wait_ge(ready_pool, 1)
        for dst, src in setup_loads():
            sp.dma_start(dst, src).then_inc(loaded, 16)
        for L in range(LANES):
            sp.dma_start(x_in[L][:], a["x"][L].rearrange("(t p) e -> p t e", p=P)).then_inc(x_loaded[L], 16)
        with sp.Fori(0, loops - 1) as i:
            for L in range(LANES):
                sp.wait_ge(*is_filled(L, i, "x"))
                sp.dma_start(x_in[L][:], a["x"][bass.ds(LANES * i + LANES + L, 1)].rearrange(
                    "o (t p) e -> p (o t) e", p=P)).then_inc(x_loaded[L], 16)
            for L in range(LANES):
                sp.wait_ge(*is_taken(L, i, "out"))
                sp.dma_start(out[bass.ds(LANES * i + L, 1)].rearrange("o (t p) e -> p (o t) e", p=P),
                             x_out[L][:]).then_inc(x_stored[L], 16)
        for L in range(LANES):
            sp.wait_ge(*is_taken(L, loops - 1, "out"))
            sp.dma_start(out[n_batch - LANES + L].rearrange("(t p) e -> p t e", p=P),
                         x_out[L][:]).then_inc(x_stored[L], 16)
        for L in range(LANES):
            sp.wait_ge(x_stored[L], 16 * loops + 1)

    @block.gpsimd
    def _(pool):
        g = nc.gpsimd
        for l in range(2):
            g.memset(w_nat[l][:, 0:3 * P], 0.0)
        for L in range(LANES):
            last = g.memset(shifted[L][:, 0:1], 0.0)
        last.then_inc(ready_pool, 1)
        pool.wait_ge(ready_dve, SETUP_DVE)

        def rope_b(L, i, l):
            for u in range(4):
                pool.wait_ge(s_qkcs[L], i * 4 * DEPTH + 4 * l + u + 1)
                g.tensor_tensor(qk_cos[L][:, u, :], qk_cos[L][:, u, :], qk_sin[L][:, u % 2, :],
                                ALU.add).then_inc(s_rotsum[L], 1)
            pool.wait_ge(s_rnorm[L], i * DEPTH + l + 1)
            for u in range(4):
                pool.wait_ge(s_rotsum[L], i * 4 * DEPTH + 4 * l + u + 1)
                r = qk_cos[L][:, u, :].rearrange("p (h d) -> p h d", d=DH)
                g.tensor_tensor(r, r, qk_rn[L][:, u, :].unsqueeze(2).broadcast_to([P, HEADS, DH]),
                                ALU.mult).then_inc(s_rot[L], 1)

        def rope_c_heads(L, i):
            pool.wait_ge(s_ropec[L], 2 * i + 1)
            g.tensor_tensor(k_c[L][:, 0, :], k_c[L][:, 0, :], k_c[L][:, 1, :], ALU.add).then_inc(s_qkc[L], 1)
            pool.wait_ge(s_ropec[L], 2 * i + 2)
            pool.wait_ge(s_qkc[L], 2 * i + 1)
            g.tensor_tensor(q_c[L][:, 0, :], q_c[L][:, 0, :], q_c[L][:, 1, :], ALU.add).then_inc(s_qkc[L], 1)
            for h in range(CHEADS):
                g.tensor_scalar(k_heads[L][:, h, :], k_c[L][:, 0, :], head_rows[:, h:h + 1], 1.0,
                                ALU.mult, ALU.mult).then_inc(s_kheads[L], 1)

        with pool.Fori(0, loops) as i:
            for L in range(LANES):
                pool.wait_ge(taken[L][place["D.out"][0]], i * per_batch[place["D.out"][0]] + 1)
                g.tensor_copy(mod[L][:], mod_t[:, bass.ds(LANES * i + L, 1), :].rearrange(
                    "p o m -> p (o m)")).then_inc(mod_ready[L], 1)
            for l in range(DEPTH):
                for L in range(LANES):
                    rope_b(L, i, l)
            for L in range(LANES):
                rope_c_heads(L, i)

    @block.tensor
    def _(pe):
        mm, tp = nc.tensor.matmul, nc.tensor.transpose
        pe.wait_ge(loaded, ALL_LOADED)
        pe.wait_ge(ready_act, 1)
        for l in range(2):
            for j in range(N_MOD):
                last = mm(bank[0][l][:, j * n_batch:(j + 1) * n_batch], w_mod[l][:, j * P:(j + 1) * P],
                          c_t[:, l, :], start=True, stop=True)
        last.then_inc(ready_pe, 1)
        pe.wait_ge(ready_dve, FP4_WEIGHTS_READY)
        for l in range(2):
            for c in range(3):
                last = tp(bank[0][2 + l][:, c * P:(c + 1) * P], w_nat[l][:, c * P:(c + 1) * P], ident[:])
        for c, rows in enumerate(FF_ROWS):
            last = tp(bank[1][0][0:rows, c * P:(c + 1) * P], ff_h[1][:, c * P:c * P + rows], ident[:])
        last.then_inc(ready_pe, 1)
        pe.wait_ge(ready_dve, SETUP_DVE)
        pe.wait_ge(ready_act, SETUP_ACT)

        def norm(L, i, k, src):
            pe.wait_ge(*is_free(L, i, f"mean{k}"))
            mm(ps(L, f"mean{k}")[:, 0:T], mean_w[:], src, start=True, stop=True).then_inc(sem_filled(L, f"mean{k}"), 1)
            pe.wait_ge(s_square[L], i * N_LN + k + 1)
            pe.wait_ge(*is_free(L, i, f"var{k}"))
            mm(ps(L, f"var{k}")[:, 0:T], mean_w[:], square[L][:], start=True, stop=True).then_inc(
                sem_filled(L, f"var{k}"), 1)

        def scores(L, i, core, first, h):
            name = f"S{first + h}"
            s = ps(L, name)
            pe.wait_ge(*is_free(L, i, name))
            if core == "C":
                pe.wait_ge(s_kheads[L], i * CHEADS + h + 1)
                for t in range(NT):
                    last = mm(s[:, t * T:(t + 1) * T], q_c[L][:, 0, t * P:(t + 1) * P], k_heads[L][:, h, :],
                              start=True, stop=True)
            else:
                rows, c = slice(DH * (h % 2), DH * (h % 2) + DH), h // 2
                for t, at in ((0, slice(0, P)), (1, slice(P, 3 * P))):
                    mm(s[:, at], ident_bf[:], mask_bf[:, 0 if core == "A" else 1, at], start=True, stop=False)
                    last = mm(s[:, at], qT[L][rows, c, t * P:(t + 1) * P], kT[L][rows, c, 0:(t + 1) * P],
                              start=False, stop=True)
            last.then_inc(sem_filled(L, name), 1)

        def blocks_of(core):
            return [(0, 0), (0, 1), (1, 0), (1, 1)] if core == "C" else [(0, 0), (1, 0), (1, 1)]

        def turn_probs(L, i, core, g):
            pe.wait_ge(*is_taken(L, i, f"S{g}"))
            pe.wait_ge(*is_free(L, i, f"P{g}"))
            for n in range(len(blocks_of(core))):
                last = tp(ps(L, f"P{g}")[:, n * P:(n + 1) * P], probs[L][:, g % 2, n * P:(n + 1) * P], ident[:])
            last.then_inc(sem_filled(L, f"P{g}"), 1)

        def weighted_values(L, i, core, first, h):
            g = first + h
            group, v, w = (CHEADS, v_c[L], CDH + 1) if core == "C" else (2, v_ab[L], DH + 1)
            name = f"O{first + h - h % group}"
            pe.wait_ge(*is_taken(L, i, f"P{g}"))
            if h % group == 0:
                pe.wait_ge(*is_free(L, i, name))
            blocks = blocks_of(core)
            for t in range(NT):
                at = (h % group * NT + t) * w
                mine = [n for n, (q, _) in enumerate(blocks) if q == t]
                for n in mine:
                    last = mm(ps(L, name)[:, at:at + w], probsT[L][:, g % 2, n * P:(n + 1) * P],
                              v[:, blocks[n][1], h, :], start=(n == mine[0]), stop=(n == mine[-1]),
                              skip_group_check=True)
            if h % group == group - 1:
                last.then_inc(sem_filled(L, name), 1)

        def attention(i, core, first, heads):
            for h in range(heads + 2):
                for L in range(LANES):
                    if h < heads:
                        scores(L, i, core, first, h)
                    if 1 <= h <= heads:
                        turn_probs(L, i, core, first + h - 1)
                    if h >= 2:
                        weighted_values(L, i, core, first, h - 2)

        def out_projection(L, i, tag, w, n_o):
            pe.wait_ge(s_o[L], i * N_NORMS + n_o)
            for t in range(NT):
                name = f"{tag}.oT{t}"
                pe.wait_ge(*is_free(L, i, name))
                for c in range(CHUNKS):
                    last = tp(ps(L, name)[:, c * P:(c + 1) * P], o[L][:, t, c * P:(c + 1) * P], ident[:])
                last.then_inc(sem_filled(L, name), 1)
            pe.wait_ge(*is_free(L, i, f"{tag}.out"))
            for t in range(NT):
                pe.wait_ge(*is_taken(L, i, f"{tag}.oT{t}"))
            for c in range(CHUNKS):
                last = mm(ps(L, f"{tag}.out")[:, 0:T], w[:, c, :], oT[L][:, c, :], start=(c == 0), stop=(c == CHUNKS - 1))
            last.then_inc(sem_filled(L, f"{tag}.out"), 1)

        def tokens_by_features(L, i, name, src, w):
            t = int(name[-1])
            pe.wait_ge(*is_free(L, i, name))
            mm(ps(L, name)[:, 0:w.shape[-1]], src[:, t * P:(t + 1) * P], w, start=True, stop=True).then_inc(
                sem_filled(L, name), 1)

        with pe.Fori(0, loops) as i:
            for L in range(LANES):
                pe.wait_ge(x_loaded[L], 16 * i + 16)
                pe.wait_ge(*is_free(L, i, "x"))
                for t in range(NT):
                    last = tp(ps(L, "x")[:, t * P:(t + 1) * P], x_in[L][:, t, :], ident[:])
                last.then_inc(sem_filled(L, "x"), 1)
            for L in range(LANES):
                pe.wait_ge(s_x[L], 5 * i + 1)
                norm(L, i, 0, xT[L][:])
            for L in range(LANES):
                pe.wait_ge(s_h[L], N_LN * i + 1)
                for n, name in enumerate(("A.q0", "A.q1", "A.k0", "A.k1")):
                    pe.wait_ge(*is_free(L, i, name))
                    for c in range(2):
                        at = (2 * n + c) * P
                        last = mm(ps(L, name)[:, c * T:(c + 1) * T], wqkv_a[:, at:at + P], hT[L][:], start=True, stop=True)
                    last.then_inc(sem_filled(L, name), 1)
                for t in range(NT):
                    tokens_by_features(L, i, f"A.v{t}", hT[L], wqkv_a[:, 2 * INNER:3 * INNER])
            for L in range(LANES):
                for name in ("A.k0", "A.k1", "A.v0", "A.v1"):
                    pe.wait_ge(*is_taken(L, i, name))
            attention(i, "A", 0, HEADS)
            for L in range(LANES):
                out_projection(L, i, "A", wo_a, HEADS // 2)
            for L in range(LANES):
                pe.wait_ge(s_x[L], 5 * i + 2)
                norm(L, i, 1, xT[L][:])
            for l in range(DEPTH):
                tag, first = CORES[1 + l][0:2]
                for L in range(LANES):
                    pe.wait_ge(s_shift[L], 4 * i + 2 * l + 1)
                    for n, what in enumerate("qkv"):
                        for t in range(NT):
                            tokens_by_features(L, i, f"{tag}.{what}{t}", shifted[L],
                                               wqkv_b[:, l, n * INNER:(n + 1) * INNER])
                for L in range(LANES):
                    for u, name in enumerate(("qT0", "qT1", "kT0", "kT1")):
                        pe.wait_ge(s_rot[L], i * 4 * DEPTH + 4 * l + u + 1)
                        pe.wait_ge(*is_free(L, i, f"{tag}.{name}"))
                        for c in range(CHUNKS):
                            last = tp(ps(L, f"{tag}.{name}")[:, c * P:(c + 1) * P],
                                      qk_cos[L][:, u, c * P:(c + 1) * P], ident[:])
                        last.then_inc(sem_filled(L, f"{tag}.{name}"), 1)
                for L in range(LANES):
                    for name in ("qT0", "qT1", "kT0", "kT1"):
                        pe.wait_ge(*is_taken(L, i, f"{tag}.{name}"))
                attention(i, tag, first, HEADS)
                for L in range(LANES):
                    out_projection(L, i, tag, wo_b[:, l], (2 + l) * HEADS // 2)
                for L in range(LANES):
                    pe.wait_ge(s_shift[L], 4 * i + 2 * l + 2)
                    norm(L, i, 2 + l, shifted[L][:, 0:T])
                for L in range(LANES):
                    pe.wait_ge(s_h[L], N_LN * i + 3 + l)
                    for name, cols, at in (("g01", HID, (0, 1)), ("g2", HID, (2,)), ("a01", 0, (0, 1)), ("a2", 0, (2,))):
                        pe.wait_ge(*is_free(L, i, f"{tag}.{name}"))
                        for n, c in enumerate(at):
                            last = mm(ps(L, f"{tag}.{name}")[0:HID_ROWS[c], n * T:(n + 1) * T],
                                      w1[:, l, cols + c * P:cols + c * P + HID_ROWS[c]], hT[L][:],
                                      start=True, stop=True)
                        last.then_inc(sem_filled(L, f"{tag}.{name}"), 1)
                for L in range(LANES):
                    pe.wait_ge(*is_free(L, i, f"{tag}.y"))
                    for c, rows in enumerate(HID_ROWS):
                        pe.wait_ge(s_hid[L], i * 3 * DEPTH + 3 * l + c + 1)
                        last = mm(ps(L, f"{tag}.y")[:, 0:T], w2[0:rows, l, c, :], hid[L][0:rows, c, :],
                                  start=(c == 0), stop=(c == 2))
                    last.then_inc(sem_filled(L, f"{tag}.y"), 1)
            for L in range(LANES):
                pe.wait_ge(s_x[L], 5 * i + 3)
                norm(L, i, 4, xT[L][:])
            for L in range(LANES):
                pe.wait_ge(s_h[L], N_LN * i + 5)
                for name, n in (("C.k", 2), ("C.q", 0)):
                    pe.wait_ge(*is_free(L, i, name))
                    for r in range(2):
                        last = mm(ps(L, name)[:, r * T:(r + 1) * T], w_c[:, n + r, :], hT[L][:], start=True, stop=True)
                    last.then_inc(sem_filled(L, name), 1)
                pe.wait_ge(*is_free(L, i, "C.v"))
                for t in range(NT):
                    last = mm(ps(L, "C.v")[:, t * P:(t + 1) * P], hT[L][:, t * P:(t + 1) * P], w_c[:, 4, :],
                              start=True, stop=True)
                last.then_inc(sem_filled(L, "C.v"), 1)
            for L in range(LANES):
                pe.wait_ge(s_qkc[L], 2 * i + 2)
                pe.wait_ge(*is_taken(L, i, "C.v"))
            attention(i, "C", 3 * HEADS, CHEADS)
            for L in range(LANES):
                pe.wait_ge(s_o[L], N_NORMS * (i + 1))
                pe.wait_ge(*is_free(L, i, "C.oT"))
                for t in range(NT):
                    last = tp(ps(L, "C.oT")[:, t * P:(t + 1) * P], o[L][:, t, 0:P], ident[:])
                last.then_inc(sem_filled(L, "C.oT"), 1)
                pe.wait_ge(*is_taken(L, i, "C.oT"))
                pe.wait_ge(*is_free(L, i, "C.out"))
                mm(ps(L, "C.out")[:, 0:T], w_c[:, 5, :], oT[L][:, 0, :], start=True, stop=True).then_inc(
                    sem_filled(L, "C.out"), 1)
            for L in range(LANES):
                pe.wait_ge(s_x[L], 5 * i + 4)
                norm(L, i, 5, xT[L][:])
            for L in range(LANES):
                pe.wait_ge(s_h[L], N_LN * i + 6)
                pe.wait_ge(*is_free(L, i, "D.h"))
                for t in range(NT):
                    last = tp(ps(L, "D.h")[:, t * P:(t + 1) * P], hT[L][:, t * P:(t + 1) * P], ident[:])
                last.then_inc(sem_filled(L, "D.h"), 1)
            for L in range(LANES):
                pe.wait_ge(s_q4[L], 2 * QSTEPS * i + QSTEPS)
                pe.wait_ge(*is_free(L, i, "D.xT"))
                for t in range(NT):
                    last = tp(ps(L, "D.xT")[:, t * P:(t + 1) * P], ff_h[L][:, t * P:(t + 1) * P], ident[:])
                last.then_inc(sem_filled(L, "D.xT"), 1)
                pe.wait_ge(*is_taken(L, i, "D.xT"))
                for w, what in ((wg_q, "g"), (wu_q, "u")):
                    for t in range(NT):
                        tokens_by_features(L, i, f"D.{what}{t}", oT[L][:, 0, :], w[:])
            for L in range(LANES):
                pe.wait_ge(s_q4[L], 2 * QSTEPS * i + 2 * QSTEPS)
                for t in range(NT):
                    pe.wait_ge(*is_free(L, i, f"D.hT{t}"))
                    for c, rows in enumerate(FF_ROWS):
                        at = t * FF + c * P
                        last = tp(ps(L, f"D.hT{t}")[0:rows, c * P:(c + 1) * P], ff_h[L][:, at:at + rows], ident[:])
                    last.then_inc(sem_filled(L, f"D.hT{t}"), 1)
                pe.wait_ge(*is_free(L, i, "D.out"))
                for t in range(NT):
                    pe.wait_ge(*is_taken(L, i, f"D.hT{t}"))
                for c, rows in enumerate(FF_ROWS):
                    last = mm(ps(L, "D.out")[:, 0:T], wd_q[0:rows, c, :], hT_q[L][0:rows, c, :],
                              start=(c == 0), stop=(c == 2))
                last.then_inc(sem_filled(L, "D.out"), 1)
            for L in range(LANES):
                pe.wait_ge(s_x[L], 5 * i + 5)
                pe.wait_ge(*is_free(L, i, "out"))
                for t in range(NT):
                    last = tp(ps(L, "out")[:, t * P:(t + 1) * P], xT[L][:, t * P:(t + 1) * P], ident[:])
                last.then_inc(sem_filled(L, "out"), 1)

    @block.scalar
    def _(act):
        f = nc.scalar.activation
        act.wait_ge(loaded, ALL_LOADED)
        f(c_t[:], c_t[:], ACT.Silu).then_inc(ready_act, 1)
        f(wqkv_a[:, 0:INNER], wqkv_a[:, 0:INNER], ACT.Copy, scale=DH ** -0.5).then_inc(ready_act, 1)
        act.wait_ge(ready_dve, SETUP_DVE)

        def exp_and_log_tables():
            nc.scalar.add_instruction(mybir.InstLoadActFuncSet(
                name=nc.get_next_instruction_name(), act_func_set_id=EXP_LN_SET, engine=mybir.EngineType.Activation))

        def norm(L, i, k, gain, bias, dst):
            act.wait_ge(s_centred[L], i * N_LN + k + 1)
            f(square[L][:], centred[L][:], ACT.Square).then_inc(s_square[L], 1)
            act.wait_ge(*is_filled(L, i, f"var{k}"))
            f(rstd[L][:], ps(L, f"var{k}")[:, 0:T], ACT.Ln, bias=eps_col[:]).then_inc(s_logvar[L], 1)
            act.wait_ge(s_logvar[L], i * N_LN + k + 1)
            f(rstd[L][:], rstd[L][:], ACT.Exp, scale=-0.5).then_inc(s_rstd[L], 1)
            act.wait_ge(s_rstd[L], i * N_LN + k + 1)
            f(square[L][:], rstd[L][:], ACT.Square).then_inc(s_rstd2[L], 1)
            act.wait_ge(s_normed[L], i * N_LN + k + 1)
            f(dst, centred[L][:], ACT.Identity, bias=bias, scale=gain).then_inc(s_h[L], 1)

        def exps(L, i, core, g):
            name = f"S{g}"
            act.wait_ge(s_max[L], i * N_MAX + maxima(g))
            wide = (T, 2 * T) if core == "C" else (P, 3 * P)
            at = 0
            for t in range(NT):
                last = f(probs[L][:, g % 2, at:wide[t]], ps(L, name)[:, at:wide[t]], ACT.Exp,
                         bias=negmax[L][:, g % 2, t:t + 1])
                at = wide[t]
            last.then_inc(sem_taken(L, name), 1)

        def probs_turned(L, i, core, g):
            n = 2 * T if core == "C" else 3 * P
            act.wait_ge(*is_filled(L, i, f"P{g}"))
            f(probsT[L][:, g % 2, 0:n], ps(L, f"P{g}")[:, 0:n], ACT.Copy).then_inc(sem_taken(L, f"P{g}"), 1)

        def attention(i, core, first, heads):
            for h in range(heads + 1):
                for L in range(LANES):
                    if h < heads:
                        exps(L, i, core, first + h)
                    if h >= 1:
                        probs_turned(L, i, core, first + h - 1)

        def values(L, i, tag):
            for t in range(NT):
                act.wait_ge(*is_filled(L, i, f"{tag}.v{t}"))
                f(v_ab[L][:, t, :, 0:DH], ps(L, f"{tag}.v{t}")[:].rearrange("p (h d) -> p h d", d=DH),
                  ACT.Copy).then_inc(sem_taken(L, f"{tag}.v{t}"), 1)

        def out_turned(L, i, tag):
            for t in range(NT):
                act.wait_ge(*is_filled(L, i, f"{tag}.oT{t}"))
                f(oT[L][:, :, t * P:(t + 1) * P], ps(L, f"{tag}.oT{t}")[:].rearrange("p (c n) -> p c n", c=CHUNKS),
                  ACT.Copy).then_inc(sem_taken(L, f"{tag}.oT{t}"), 1)

        def mod_col(L, n):
            return mod[L][:, n:n + 1]

        with act.Fori(0, loops) as i:
            exp_and_log_tables()
            for L in range(LANES):
                act.wait_ge(mod_ready[L], i + 1)
                norm(L, i, 0, mod_col(L, 1), mod_col(L, 0), hT[L][:])
            for L in range(LANES):
                values(L, i, "A")
            attention(i, "A", 0, HEADS)
            for L in range(LANES):
                out_turned(L, i, "A")
            for L in range(LANES):
                norm(L, i, 1, mod_col(L, 4), mod_col(L, 3), yT[L][:])
            for l in range(DEPTH):
                tag, first = CORES[1 + l][0:2]
                for L in range(LANES):
                    for u, name in enumerate(("q0", "q1", "k0", "k1")):
                        n = i * 4 * DEPTH + 4 * l + u
                        act.wait_ge(*is_filled(L, i, f"{tag}.{name}"))
                        if u >= 2:
                            act.wait_ge(s_ss[L], n - 1)
                        f(qk_sq[L][:, u % 2, :], ps(L, f"{tag}.{name}")[:], ACT.Square).then_inc(s_qksq[L], 1)
                    values(L, i, tag)
                    act.wait_ge(s_ssclamp[L], i * DEPTH + l + 1)
                    f(qk_rn[L][:], qk_ss[L][:], ACT.Ln, scale=SS_SCALE).then_inc(s_logss[L], 1)
                    act.wait_ge(s_logss[L], i * DEPTH + l + 1)
                    f(qk_rn[L][:], qk_rn[L][:], ACT.Exp, scale=-0.5, bias=ss_bias[:]).then_inc(s_rnorm0[L], 1)
                for L in range(LANES):
                    for dst, what in ((qT[L], "qT"), (kT[L], "kT")):
                        for t in range(NT):
                            name = f"{tag}.{what}{t}"
                            act.wait_ge(*is_filled(L, i, name))
                            f(dst[:, :, t * P:(t + 1) * P], ps(L, name)[:].rearrange("p (c n) -> p c n", c=CHUNKS),
                              ACT.Copy).then_inc(sem_taken(L, name), 1)
                attention(i, tag, first, HEADS)
                for L in range(LANES):
                    out_turned(L, i, tag)
                for L in range(LANES):
                    norm(L, i, 2 + l, ln_g[:, l:l + 1], ln_b[:, l:l + 1], hT[L][:])
                for L in range(LANES):
                    for name, at in (("g01", (0, 1)), ("g2", (2,))):
                        act.wait_ge(*is_filled(L, i, f"{tag}.{name}"))
                        for n, c in enumerate(at):
                            rows = HID_ROWS[c]
                            last = f(gelu[L][0:rows, c, :], ps(L, f"{tag}.{name}")[0:rows, n * T:(n + 1) * T], ACT.Gelu,
                                     bias=b1g[0:rows, l, c:c + 1])
                        last.then_inc(sem_taken(L, f"{tag}.{name}"), 1)
                exp_and_log_tables()
            for L in range(LANES):
                norm(L, i, 4, mod_col(L, N_MOD + 1), mod_col(L, N_MOD), hT[L][:])
            for L in range(LANES):
                act.wait_ge(*is_filled(L, i, "C.v"))
                f(v_c[L][:, :, :, 0:CDH], ps(L, "C.v")[:, 0:T].rearrange("p (t h d) -> p t h d", t=NT, d=CDH),
                  ACT.Copy).then_inc(sem_taken(L, "C.v"), 1)
            attention(i, "C", 3 * HEADS, CHEADS)
            for L in range(LANES):
                act.wait_ge(*is_filled(L, i, "C.oT"))
                f(oT[L][:, 0, :], ps(L, "C.oT")[:, 0:T], ACT.Copy).then_inc(sem_taken(L, "C.oT"), 1)
            for L in range(LANES):
                norm(L, i, 5, mod_col(L, N_MOD + 4), mod_col(L, N_MOD + 3), hT[L][:])
            for L in range(LANES):
                act.wait_ge(*is_filled(L, i, "D.xT"))
                f(oT[L][:, 0, :], ps(L, "D.xT")[:, 0:T], ACT.Copy).then_inc(sem_taken(L, "D.xT"), 1)
            for L in range(LANES):
                for t in range(NT):
                    act.wait_ge(*is_filled(L, i, f"D.g{t}"))
                    f(ff_a[L][:, t * FF:(t + 1) * FF], ps(L, f"D.g{t}")[:, 0:FF], ACT.Silu).then_inc(
                        sem_taken(L, f"D.g{t}"), 1)
            for L in range(LANES):
                for t in range(NT):
                    act.wait_ge(*is_filled(L, i, f"D.hT{t}"))
                    for c, rows in enumerate(FF_ROWS):
                        last = f(hT_q[L][0:rows, c, t * P:(t + 1) * P], ps(L, f"D.hT{t}")[0:rows, c * P:(c + 1) * P],
                                 ACT.Copy)
                    last.then_inc(sem_taken(L, f"D.hT{t}"), 1)
            for L in range(LANES):
                act.wait_ge(*is_filled(L, i, "out"))
                act.wait_ge(x_stored[L], 16 * i + 1)
                f(x_out[L][:], ps(L, "out")[:, 0:T].rearrange("p (t e) -> p t e", t=NT), ACT.Copy).then_inc(
                    sem_taken(L, "out"), 1)

    @block.vector
    def _(dve):
        v = nc.vector
        done = 0
        v.memset(mean_w[:], 1.0 / P)
        v.memset(eps_col[:], 1e-5)
        v.memset(ss_bias[:], 0.5 * math.log(SS_SCALE))
        for L in range(LANES):
            for b in range(4):
                v.engine_nop().then_inc(taken[L][b], 1)
            v.engine_nop().then_inc(x_stored[L], 1)
            v.memset(v_ab[L][:, :, :, DH:DH + 1], 1.0)
            v.memset(v_c[L][:, :, :, CDH:CDH + 1], 1.0)
        dve.wait_ge(loaded, ALL_LOADED)
        v.tensor_copy(ident_bf[:], ident[:])
        v.tensor_copy(mask_bf[:], masks)
        for l in range(DEPTH):
            for t in range(NT):
                v.tensor_tensor(xpos[:, l, t], xpos[:, l, t], head_scale[:, l], ALU.mult)
        dve.wait_ge(ready_pe, 1)
        for l in range(2):
            m = bank[0][l][:, 0:N_MOD * n_batch].rearrange("p (j b) -> p b j", j=N_MOD)
            out_m = mod_t[:, :, l * N_MOD:(l + 1) * N_MOD]
            last = v.tensor_copy(out_m, m)
        last.then_inc(ready_dve, 1)
        dve.wait_ge(ready_dve, 1)
        gates = mod_t[:].rearrange("p b (g j) -> p b g j", j=3)
        sign = qk_sin[0][:, 0, 0:4 * n_batch].rearrange("p (b g) -> p b g", g=4)
        size = qk_sin[0][:, 1, 0:4 * n_batch].rearrange("p (b g) -> p b g", g=4)
        v.tensor_scalar(gates[:, :, :, 1], gates[:, :, :, 1], 1.0, None, ALU.add)
        v.tensor_scalar(sign, gates[:, :, :, 2], 0.0, 2.0, ALU.is_ge, ALU.mult)
        v.tensor_copy(size, gates[:, :, :, 2]).then_inc(ready_dve, 1)
        dve.wait_ge(ready_dve, 2)
        v.scalar_tensor_tensor(size, size, -1.0, size, ALU.mult, ALU.max).then_inc(ready_dve, 1)
        dve.wait_ge(ready_dve, 3)
        v.tensor_scalar(size, size, 0.25, None, ALU.max).then_inc(ready_dve, 1)
        dve.wait_ge(ready_dve, 4)
        v.scalar_tensor_tensor(sign, sign, -1.0, size, ALU.add, ALU.mult).then_inc(ready_dve, 1)
        dve.wait_ge(ready_dve, 5)
        v.tensor_copy(gates[:, :, :, 2], sign).then_inc(ready_dve, 1)
        for n, (w, cols, L) in enumerate(((w_nat[0], 3 * P, 0), (w_nat[1], 3 * P, 0), (ff_h[1], FF, 0))):
            base = MOD_READY + n * QSTEPS
            dve.wait_ge(ready_dve, base)
            fp4(dve, w[:, 0:cols], w[:, 0:cols], L, ready_dve, base, cols)
        dve.wait_ge(ready_pe, 2)
        v.tensor_copy(wg_q[:], bank[0][2][:, 0:FF])
        v.tensor_copy(wu_q[:], bank[0][3][:, 0:FF])
        for c, rows in enumerate(FF_ROWS):
            last = v.tensor_copy(wd_q[0:rows, c, :], bank[1][0][0:rows, c * P:(c + 1) * P])
        last.then_inc(ready_dve, 1)

        def norm(L, i, k, src):
            dve.wait_ge(*is_filled(L, i, f"mean{k}"))
            v.tensor_tensor(centred[L][:], src, ps(L, f"mean{k}")[:, 0:T], ALU.subtract).then_inc(
                s_centred[L], 1)
            v.engine_nop().then_inc(sem_taken(L, f"mean{k}"), 1)
            n = 3 * (i * N_LN + k)
            dve.wait_ge(s_rstd2[L], i * N_LN + k + 1)
            v.scalar_tensor_tensor(square[L][:], ps(L, f"var{k}")[:, 0:T], 1e-5, square[L][:], ALU.add,
                                   ALU.mult).then_inc(s_newton[L], 1)
            v.tensor_tensor(centred[L][:], centred[L][:], rstd[L][:], ALU.mult).then_inc(s_newton[L], 1)
            dve.wait_ge(s_newton[L], n + 1)
            v.tensor_scalar(square[L][:], square[L][:], -0.5, 1.5, ALU.mult, ALU.add).then_inc(s_newton[L], 1)
            v.engine_nop().then_inc(sem_taken(L, f"var{k}"), 1)
            dve.wait_ge(s_newton[L], n + 3)
            v.tensor_tensor(centred[L][:], centred[L][:], square[L][:], ALU.mult).then_inc(s_normed[L], 1)

        def row_max(L, i, core, g):
            name = f"S{g}"
            dve.wait_ge(*is_filled(L, i, name))
            if core == "C":
                v.tensor_reduce(negmax[L][:, g % 2, :], ps(L, name)[:].rearrange("p (t n) -> p t n", t=NT), AX_X,
                                ALU.max, negate=True).then_inc(s_max[L], 1)
            else:
                v.tensor_reduce(negmax[L][:, g % 2, 0:1], ps(L, name)[:, 0:P], AX_X, ALU.max,
                                negate=True).then_inc(s_max[L], 1)
                v.tensor_reduce(negmax[L][:, g % 2, 1:2], ps(L, name)[:, P:3 * P], AX_X, ALU.max,
                                negate=True).then_inc(s_max[L], 1)

        def normalise(L, i, core, first, h, n_norm):
            group, w = (CHEADS, CDH + 1) if core == "C" else (2, DH + 1)
            name = f"O{first + h - group + 1}"
            dve.wait_ge(*is_filled(L, i, name))
            acc = ps(L, name)[:, 0:group * NT * w].rearrange("p (h t w) -> p h t w", t=NT, w=w)
            recip = rz[L][:, 0:group * NT].rearrange("p (h t) -> p h t", t=NT)
            v.reciprocal(recip, acc[:, :, :, w - 1]).then_inc(s_rz[L], 1)
            dve.wait_ge(s_rz[L], i * N_NORMS + n_norm + 1)
            d = w - 1
            for t in range(NT):
                dst = o[L][:, t, (h - group + 1) * d:(h + 1) * d].rearrange("p (h d) -> p h d", d=d)
                last = v.tensor_tensor(dst, acc[:, :, t, 0:d], recip[:, :, t].unsqueeze(2).broadcast_to([P, group, d]),
                                       ALU.mult)
            last.then_inc(s_o[L], 1)
            v.engine_nop().then_inc(sem_taken(L, name), 1)

        def attention(i, core, first, heads, n_norm):
            group = CHEADS if core == "C" else 2
            for h in range(heads + 2):
                for L in range(LANES):
                    if h < heads:
                        row_max(L, i, core, first + h)
                    if h >= 2 and (h - 2) % group == group - 1:
                        normalise(L, i, core, first, h - 2, n_norm + (h - 2) // group)

        def shift(L, i, n_y, n):
            dve.wait_ge(s_y[L] if n_y else s_h[L], 4 * i + n_y if n_y else i * N_LN + 2)
            v.tensor_copy(shifted[L][0:P // 2, 0:T], yT[L][0:P // 2, :])
            v.tensor_copy(shifted[L][P // 2:P, 1:T + 1], yT[L][P // 2:P, :]).then_inc(s_shift[L], 1)

        with dve.Fori(0, loops) as i:
            for L in range(LANES):
                dve.wait_ge(*is_filled(L, i, "x"))
                v.tensor_copy(xT[L][:], ps(L, "x")[:, 0:T]).then_inc(s_x[L], 1)
                v.engine_nop().then_inc(sem_taken(L, "x"), 1)
            for L in range(LANES):
                dve.wait_ge(s_x[L], 5 * i + 1)
                norm(L, i, 0, xT[L][:])
            for L in range(LANES):
                for dst, pe_t, what in ((qT[L], pe_q, "q"), (kT[L], pe_k, "k")):
                    for n in range(2):
                        name = f"A.{what}{n}"
                        dve.wait_ge(*is_filled(L, i, name))
                        v.tensor_tensor(dst[:, 2 * n:2 * n + 2, :], ps(L, name)[:].rearrange("p (c t) -> p c t", c=2),
                                        pe_t[:].unsqueeze(1).broadcast_to([P, 2, T]), ALU.add).then_inc(
                                            sem_taken(L, name), 1)
            attention(i, "A", 0, HEADS, 0)
            for L in range(LANES):
                dve.wait_ge(*is_filled(L, i, "A.out"))
                v.scalar_tensor_tensor(xT[L][:], ps(L, "A.out")[:, 0:T], mod[L][:, 2:3], xT[L][:],
                                       ALU.mult, ALU.add).then_inc(s_x[L], 1)
                v.engine_nop().then_inc(sem_taken(L, "A.out"), 1)
            for L in range(LANES):
                dve.wait_ge(s_x[L], 5 * i + 2)
                norm(L, i, 1, xT[L][:])
            for l in range(DEPTH):
                tag, first = CORES[1 + l][0:2]
                for L in range(LANES):
                    shift(L, i, 2 * l, 2 * l)
                for L in range(LANES):
                    for u, name in enumerate(("q0", "q1", "k0", "k1")):
                        at = i * 4 * DEPTH + 4 * l + u
                        t, which = u % 2, u // 2
                        src = ps(L, f"{tag}.{name}")[:].rearrange("p (h d) -> p h d", d=DH)
                        dve.wait_ge(s_qksq[L], at + 1)

                        def table(n, lo, hi):
                            return xpos[:, l, t, n, lo:hi].unsqueeze(1).broadcast_to([P, HEADS, hi - lo])

                        cos = qk_cos[L][:, u, :].rearrange("p (h d) -> p h d", d=DH)
                        sin = qk_sin[L][:, u % 2, :].rearrange("p (h d) -> p h d", d=DH)
                        half = DH // 2
                        v.tensor_tensor(cos, src, table(2 * which, 0, DH), ALU.mult)
                        if u >= 2:
                            dve.wait_ge(s_rotsum[L], at - 1)
                        v.tensor_tensor(sin[:, :, 0:half], src[:, :, half:DH], table(2 * which + 1, 0, half), ALU.mult)
                        v.tensor_tensor(sin[:, :, half:DH], src[:, :, 0:half], table(2 * which + 1, half, DH),
                                        ALU.mult).then_inc(s_qkcs[L], 1)
                        v.tensor_reduce(qk_ss[L][:, u, :], qk_sq[L][:, u % 2, :].rearrange("p (h d) -> p h d", d=DH),
                                        AX_X, ALU.add).then_inc(s_ss[L], 1)
                        v.engine_nop().then_inc(sem_taken(L, f"{tag}.{name}"), 1)
                    dve.wait_ge(s_ss[L], (i * DEPTH + l + 1) * 4)
                    v.tensor_scalar(qk_ss[L][:], qk_ss[L][:], 1e-24, None, ALU.max).then_inc(s_ssclamp[L], 1)
                    n = 3 * (i * DEPTH + l)
                    ss, y = qk_ss[L][:], qk_rn[L][:]
                    dve.wait_ge(s_rnorm0[L], i * DEPTH + l + 1)
                    v.tensor_tensor(ss, ss, y, ALU.mult).then_inc(s_rnorm_step[L], 1)
                    dve.wait_ge(s_rnorm_step[L], n + 1)
                    v.tensor_tensor(ss, ss, y, ALU.mult).then_inc(s_rnorm_step[L], 1)
                    dve.wait_ge(s_rnorm_step[L], n + 2)
                    v.tensor_scalar(ss, ss, -0.5, 1.5, ALU.mult, ALU.add).then_inc(s_rnorm_step[L], 1)
                    dve.wait_ge(s_rnorm_step[L], n + 3)
                    v.tensor_tensor(y, y, ss, ALU.mult).then_inc(s_rnorm[L], 1)
                attention(i, tag, first, HEADS, (1 + l) * HEADS // 2)
                for L in range(LANES):
                    dve.wait_ge(*is_filled(L, i, f"{tag}.out"))
                    v.tensor_tensor(yT[L][:], ps(L, f"{tag}.out")[:, 0:T], yT[L][:], ALU.add).then_inc(s_y[L], 1)
                    v.engine_nop().then_inc(sem_taken(L, f"{tag}.out"), 1)
                for L in range(LANES):
                    shift(L, i, 2 * l + 1, 2 * l + 1)
                for L in range(LANES):
                    dve.wait_ge(s_shift[L], 4 * i + 2 * l + 2)
                    norm(L, i, 2 + l, shifted[L][:, 0:T])
                for L in range(LANES):
                    for name, at in (("a01", (0, 1)), ("a2", (2,))):
                        dve.wait_ge(*is_filled(L, i, f"{tag}.{name}"))
                        dve.wait_ge(*is_taken(L, i, f"{tag}.{'g01' if at[0] == 0 else 'g2'}"))
                        for n, c in enumerate(at):
                            rows = HID_ROWS[c]
                            v.scalar_tensor_tensor(hid[L][0:rows, c, :], ps(L, f"{tag}.{name}")[0:rows, n * T:(n + 1) * T],
                                                   b1a[0:rows, l, c:c + 1], gelu[L][0:rows, c, :], ALU.add,
                                                   ALU.mult).then_inc(s_hid[L], 1)
                        v.engine_nop().then_inc(sem_taken(L, f"{tag}.{name}"), 1)
                for L in range(LANES):
                    dve.wait_ge(*is_filled(L, i, f"{tag}.y"))
                    v.scalar_tensor_tensor(yT[L][:], ps(L, f"{tag}.y")[:, 0:T], b2[:, l:l + 1], yT[L][:],
                                           ALU.add, ALU.add).then_inc(s_y[L], 1)
                    v.engine_nop().then_inc(sem_taken(L, f"{tag}.y"), 1)
            for L in range(LANES):
                dve.wait_ge(s_y[L], 4 * i + 4)
                v.scalar_tensor_tensor(xT[L][:], yT[L][:], mod[L][:, 5:6], xT[L][:], ALU.mult,
                                       ALU.add).then_inc(s_x[L], 1)
            for L in range(LANES):
                dve.wait_ge(s_x[L], 5 * i + 3)
                norm(L, i, 4, xT[L][:])
            for L in range(LANES):
                for dst, name, n in ((k_c[L], "C.k", 2), (q_c[L], "C.q", 0)):
                    dve.wait_ge(*is_filled(L, i, name))
                    v.tensor_tensor(dst[:], ps(L, name)[:].rearrange("p (r t) -> p r t", r=2), rope_c[:, n:n + 2, :],
                                    ALU.mult).then_inc(s_ropec[L], 1)
                    v.engine_nop().then_inc(sem_taken(L, name), 1)
            attention(i, "C", 3 * HEADS, CHEADS, 3 * HEADS // 2)
            for L in range(LANES):
                dve.wait_ge(*is_filled(L, i, "C.out"))
                v.scalar_tensor_tensor(xT[L][:], ps(L, "C.out")[:, 0:T], mod[L][:, N_MOD + 2:N_MOD + 3], xT[L][:],
                                       ALU.mult, ALU.add).then_inc(s_x[L], 1)
                v.engine_nop().then_inc(sem_taken(L, "C.out"), 1)
            for L in range(LANES):
                dve.wait_ge(s_x[L], 5 * i + 4)
                norm(L, i, 5, xT[L][:])
            for L in range(LANES):
                dve.wait_ge(*is_filled(L, i, "D.h"))
                fp4(dve, ps(L, "D.h")[:, 0:T], ff_h[L][:, 0:T], L, s_q4[L], 2 * QSTEPS * i, T)
                v.engine_nop().then_inc(sem_taken(L, "D.h"), 1)
            for L in range(LANES):
                for t in range(NT):
                    dve.wait_ge(*is_filled(L, i, f"D.u{t}"))
                    dve.wait_ge(*is_taken(L, i, f"D.g{t}"))
                    v.tensor_tensor(ff_h[L][:, t * FF:(t + 1) * FF], ps(L, f"D.u{t}")[:, 0:FF],
                                    ff_a[L][:, t * FF:(t + 1) * FF], ALU.mult).then_inc(sem_taken(L, f"D.u{t}"), 1)
                for t in range(NT):
                    dve.wait_ge(*is_taken(L, i, f"D.u{t}"))
                fp4(dve, ff_h[L][:], ff_h[L][:], L, s_q4[L], 2 * QSTEPS * i + QSTEPS, NT * FF)
            for L in range(LANES):
                dve.wait_ge(*is_filled(L, i, "D.out"))
                v.scalar_tensor_tensor(xT[L][:], ps(L, "D.out")[:, 0:T], mod[L][:, N_MOD + 5:N_MOD + 6], xT[L][:],
                                       ALU.mult, ALU.add).then_inc(s_x[L], 1)
                v.engine_nop().then_inc(sem_taken(L, "D.out"), 1)


MOD_READY = 6
FP4_WEIGHTS_READY = MOD_READY + 3 * QSTEPS
SETUP_DVE = FP4_WEIGHTS_READY + 1
SETUP_ACT = 2


def shape_constants():
    import numpy as np

    f = np.float32
    c = {}
    c["c_ident"] = np.eye(P, dtype=f)
    i, j = np.arange(P)[:, None], np.arange(P)[None, :]
    off = f(-1e30)
    zero = np.zeros((P, P), f)
    causal = np.where(j <= i, zero, off)
    band = np.where((j <= i) & (i <= j + WINDOW), zero, off)
    before = np.where(i + P <= j + WINDOW, zero, off)
    c["c_masks"] = np.stack([np.concatenate([causal, zero, causal], 1), np.concatenate([band, before, band], 1)])
    pos = np.arange(T, dtype=f)[:, None]
    div = np.exp(np.arange(0, DH, 2, dtype=f) * f(-np.log(10000.0) / DH)).astype(f)
    ang = (pos * div).astype(f)
    pe = np.stack([np.sin(ang), np.cos(ang)], -1).reshape(T, DH).astype(f)
    c["c_pe_k"] = np.concatenate([pe.T, pe.T], 0)
    c["c_pe_q"] = c["c_pe_k"] * f(DH ** -0.5)
    half = np.arange(0, DH, 2, dtype=f)
    inv_freq = (f(1.0) / f(10000.0) ** (half / f(DH))).astype(f)
    freqs = np.concatenate([pos * inv_freq[None]] * 2, -1).astype(f)
    base = ((half + f(0.4 * DH)) / f(1.4 * DH)).astype(f)
    power = ((pos[:, 0] - T // 2) / f(WINDOW // 2)).astype(f)
    decay = np.concatenate([base[None] ** power[:, None]] * 2, -1).astype(f)
    sign = np.concatenate([-np.ones(DH // 2, f), np.ones(DH // 2, f)])
    cos, sin = np.cos(freqs), np.sin(freqs) * sign
    c["c_xpos"] = np.stack([f(8) * cos * decay, f(8) * sin * decay, cos / decay, sin / decay], 1).reshape(
        NT, P, 4, DH).astype(f)
    fr = np.exp(f(-np.log(10000.0)) * np.arange(0, CDH, 2, dtype=f) / f(CDH)).astype(f)
    ang = (pos * fr).astype(f)
    cosc = np.tile(np.repeat(np.cos(ang).T, 2, 0), (CHEADS, 1))
    sinc = np.tile((np.stack([-np.sin(ang), np.sin(ang)], -1).reshape(T, CDH)).T, (CHEADS, 1))
    s = f(CDH ** -0.5)
    c["c_rope"] = np.stack([cosc * s, sinc * s, cosc, sinc]).astype(f)
    c["c_head_rows"] = (np.arange(P)[:, None] // CDH == np.arange(CHEADS)[None, :]).astype(f)
    return c


def laid_out(inputs):
    import numpy as np

    x = {k: np.asarray(v) for k, v in inputs.items()}
    w = x["L0_attn_Wqkv"].reshape(HEADS, 3, DH, P).transpose(1, 0, 2, 3).reshape(3 * INNER, P)
    swap = np.arange(P) ^ 1
    return {
        "x": x["L0_attn_x"],
        "wqkv_a": w.T,
        "wo_a": x["L0_attn_Wo"].T,
        "wqkv_b": x["L0_ffn_wqkv"], "wo_b": x["L0_ffn_wo"], "w1": x["L0_ffn_w1"], "w2": x["L0_ffn_w2"],
        "q_scale": x["L0_ffn_q_scale"], "k_scale": x["L0_ffn_k_scale"],
        "ln_g": x["L0_ffn_ln_g"], "ln_b": x["L0_ffn_ln_b"], "b1": x["L0_ffn_b1"], "b2": x["L0_ffn_b2"],
        "c_t": np.stack([x["L0_c"].T, x["L1_c"].T]),
        "wmod": np.stack([x["L0_wmod"], x["L1_wmod"]]),
        "w_c": np.stack([x["L1_attn_W_q"].T, x["L1_attn_W_q"][swap].T, x["L1_attn_W_k"].T,
                         x["L1_attn_W_k"][swap].T, x["L1_attn_W_v"].T, x["L1_attn_W_o"].T]),
        "w_gate": x["L1_ffn_w_gate"], "w_up": x["L1_ffn_w_up"], "w_down": x["L1_ffn_w_down"],
    }


def prepare(inputs, bacc):
    import numpy as np

    nc = bacc.Bacc("TRN2", target_bir_lowering=False, num_devices=1)
    consts = shape_constants()
    arrays, aps = {}, {}
    for name, v in {**laid_out(inputs), **consts}.items():
        v = np.ascontiguousarray(v)
        arrays[f"in_{name}"] = v
        aps[name] = nc.dram_tensor(f"in_{name}", v.shape, mybir.dt.from_np(v.dtype), kind="ExternalInput").ap()
    n_batch = aps["x"].shape[0]
    out = nc.dram_tensor("out_x", (n_batch, T, P), F32, kind="ExternalOutput").ap()
    adaln_program(nc, aps, out, n_batch)
    return nc, arrays


def kernel(**inputs):
    import concourse.bacc as bacc
    from concourse.bass_utils import run_bass_kernel_spmd

    nc, arrays = prepare(inputs, bacc)
    result = run_bass_kernel_spmd(nc, [arrays], core_ids=[0])
    return result.results[0]["out_x"]
```

```python
import math
from contextlib import ExitStack

import concourse.bass as bass
from concourse import mybir

ALU = mybir.AluOpType
ACT = mybir.ActivationFunctionType
AX_X = mybir.AxisListType.X
F32 = mybir.dt.float32
BF16 = mybir.dt.bfloat16
U32 = mybir.dt.uint32

P = 128
T = 256
NT = T // P
LANES = 2
HEADS, DH = 8, 64
INNER = HEADS * DH
CHEADS, CDH = 16, 8
CHUNKS = INNER // P
GROUP = 4
CPAD = 32
DEPTH = 2
HID = 341
HID_ROWS = [128, 128, HID - 256]
FF = 352
FF_ROWS = [128, 128, FF - 256]
BLOCK = 16
WINDOW = 64
N_LN = 6
N_HEADS = 3 * HEADS + CHEADS
N_MOD = 6
QSTEPS = 15
ROT_ON_VECTOR = (1, 3)
EXP_LN_SET = 6
SS_SCALE = 2.0 ** 17


def bank_uses():
    uses = []

    def norm(k):
        uses.extend([(f"mean{k}", 2), (f"var{k}", 3)])

    def core(first, heads, group):
        for h in range(heads + 3):
            if h < heads:
                uses.append((f"S{first + h}", (first + h) % 2))
            if 2 <= h <= heads + 1:
                uses.append((f"P{first + h - 2}", 2))
            if h >= 3 and (h - 3) % group == 0:
                uses.append((f"O{first + h - 3}", 3))

    core(0, HEADS, GROUP)
    uses += [("A.out", 2)]
    norm(1)
    for l in range(DEPTH):
        uses += [(f"B{l}.{n}", b) for n, b in (("q0", 0), ("q1", 1), ("k0", 2), ("k1", 3), ("v0", 0), ("v1", 1),
                                               ("qT0", 2), ("qT1", 3), ("kT0", 0), ("kT1", 1))]
        core(HEADS * (1 + l), HEADS, GROUP)
        uses += [(f"B{l}.out", 2)]
        norm(2 + l)
        uses += [(f"B{l}.g01", 0), (f"B{l}.g2", 1), (f"B{l}.a01", 2), (f"B{l}.a2", 3), (f"B{l}.y", 0)]
    norm(4)
    uses += [("C.q", 0), ("C.k", 1), ("C.v", 2)]
    core(3 * HEADS, CHEADS, CHEADS)
    uses += [("C.out", 1)]
    norm(5)
    uses += [("D.h", 0)]
    return uses


TURNOVER_USES = {
    ("x_in",): ["x"], ("mean", 0): ["mean0"], ("var", 0): ["var0"], ("A.qk", 0): ["A.q0"], ("A.qk", 1): ["A.q1"],
    ("A.qk", 2): ["A.k0"], ("A.qk", 3): ["A.k1"], ("v", "A", 0): ["A.v0"], ("v", "A", 1): ["A.v1"],
    ("D.xT",): ["D.xT"], ("D.gate",): ["D.g0", "D.g1"], ("D.up",): ["D.u0", "D.u1"], ("D.hT", 0): ["D.hT0"],
    ("D.hT", 1): ["D.hT1"], ("D.out",): ["D.out"], ("x_out",): ["out"]}
TURNOVER_BANKS = {
    "x": 0, "mean0": 2, "var0": 3, "A.q0": 0, "A.q1": 1, "A.k0": 2, "A.k1": 3, "A.v0": 0, "A.v1": 1,
    "D.xT": 1, "D.g0": 2, "D.g1": 3, "D.u0": 0, "D.u1": 1, "D.hT0": 2, "D.hT1": 3, "D.out": 0, "out": 1}


def turnover_uses():
    return [(name, TURNOVER_BANKS[name]) for _, phase in turnover(1) for name in TURNOVER_USES.get(phase, [])]


def count_uses(uses):
    total, place = [0] * 4, {}
    for name, b in uses:
        assert name not in place
        place[name] = (b, total[b])
        total[b] += 1
    return place, total


def norm_phases(k):
    return [("mean", k), ("centre", k), ("var", k), ("rstd", k), ("newton", k), ("norm_out", k)]


def out_phases(tag):
    return [("out", tag)]


def rotary_phases(l):
    return ([("shift", 2 * l)] + [("qk", l, u) for u in range(4)] + [("v", f"B{l}", t) for t in range(NT)]
            + [("rnorm", l)] + [("rot", l, u) for u in range(4)] + [("turn", l, u) for u in range(4)])


def geglu_phases(l):
    return [("shift", 2 * l + 1)] + norm_phases(2 + l) + [("gate", l), ("up", l), ("down", l)]


BEFORE_A = [("x_in",)] + norm_phases(0) + [("A.qk", n) for n in range(4)] + [("v", "A", t) for t in range(NT)]
BEFORE_B0 = out_phases("A") + norm_phases(1) + rotary_phases(0)
BEFORE_B1 = out_phases("B0") + geglu_phases(0) + rotary_phases(1)
BEFORE_C = (out_phases("B1") + geglu_phases(1) + [("x_of_B",)] + norm_phases(4)
            + [("C.qk",), ("C.v",), ("C.heads",)])
AFTER_C = [("C.out",)] + norm_phases(5) + [("D.h",)] + [("D.quant", 0, k) for k in range(4)]
FP4_PART = ([("D.quant", 0, k) for k in range(4, QSTEPS)] + [("D.xT",), ("D.gate",), ("D.up",)]
            + [("D.quant", 1, k) for k in range(QSTEPS)] + [("D.hT", 0), ("D.hT", 1), ("D.out",), ("x_out",)])


def phases(i, *lists):
    return [(i, phase) for phase_list in lists for phase in phase_list]


def core(i, name, heads):
    return [(i, ("core", name, part, h)) for h in range(heads + 3) for part in ("scores", "turn", "values")]


def turnover(i, missing=None):
    steps = []
    for j, phase in spread(phases(i - 1, FP4_PART), phases(i, BEFORE_A)):
        if missing is not None and j == missing:
            steps += [(j, ("no_use", name)) for name in TURNOVER_USES.get(phase, [])]
        else:
            steps.append((j, phase))
    return steps


def spread(old, new):
    out, n = [], 0
    for k, step in enumerate(old):
        while n < len(new) and n * len(old) * SPREAD <= k * len(new):
            out.append(new[n])
            n += 1
        out.append(step)
    return out + new[n:]


SPREAD = 0.8


def sequence(i):
    return [core(i, "A", HEADS), phases(i, BEFORE_B0) + core(i, "B0", HEADS),
            phases(i, BEFORE_B1) + core(i, "B1", HEADS),
            phases(i, BEFORE_C) + core(i, "C", CHEADS) + phases(i, AFTER_C)]


LEAD = [2, 1]


def joined(parts):
    return [step for part in parts for step in part]


def start_steps(L):
    return turnover(0, missing=-1) + joined(sequence(0)[:LEAD[L]])


def loop_steps(L, i):
    return joined(sequence(i)[LEAD[L]:]) + turnover(i + 1) + joined(sequence(i + 1)[:LEAD[L]])


def end_steps(L, i):
    return joined(sequence(i)[LEAD[L]:]) + turnover(i + 1, missing=i + 1)


def in_turns(turns, steps):
    at = [0, 0]
    for n, run in enumerate(turns.split()):
        L = n % LANES
        for i, step in steps[L][at[L]:at[L] + int(run)]:
            yield L, i, step
        at[L] += int(run)
    assert at == [len(s) for s in steps]


TURNS = {
    "tensor": {
        "start": "1 1 2 2 9 9 10 1 6 2 1 1 4 1 2 5 9 3 3 3 3 1 5 2 1 1 2 2 5 4 11 6 4 3 6 1 10 6 6 1 11",
        "loop": (
            "2 1 2 2 4 5 1 3 1 8 6 1 1 1 6 8 4 3 6 1 1 1 2 2 1 1 1 1 1 1 1 1 1 1 1 1 1 1 1 1 1 1 1 1 1 2 2 3 3 4 "
            "3 1 4 2 3 2 2 4 4 2 1 2 1 4 2 7 6 4 3 6 6 1 4 3 3 1 1 1 1 1 1 1 1 1 1 1 1 1 1 1 1 1 1 1 1 1 1 1 1 3 "
            "3 3 3 4 3 1 3 2 3 2 3 4 9 2 1 2 4 2 1 4 6 3 5 6 4 1 13 15 1 3 2 6 2 3 3 3 3 3 3 3 3 3 3 3 5 9 2 2 1 "
            "4 8 5 4 4 2 6 8 7 4 1 3 2 4 2 1 6 1 3 2 6 5 5 11 2 3 1 1 4 6 4 4 3 1 1 1 1 1 1 1 1 1 1 1 1 1 1 1 1 1 "
            "1 1 1 1 1 1 1 1 1 2 2 1 1 2 2 1 1 3 3 1 1"
        ),
        "end": (
            "2 1 2 2 4 5 1 5 1 6 5 1 1 1 1 1 6 8 1 2 1 1 1 1 1 5 6 4 1 1 2 4 3 3 2 4 2 1 3 2 3 2 3 4 8 4 2 5 2 6 "
            "4 10 1 3 1 1 2 3 2 3 4 9 3 4 6 4 1 4 5 4 6 2 1 2 2 2 2 4 7 3 2 6 2 6 1 1 1 2 1 1 1 1 1 1 1 2 1 1 1 1 "
            "1 2 1 1 2 3 3 3 1 2 2 1 1 3 4 3 1 3 2 4 4 10 19 26 24 24 3 2 1 2"
        ),
    },
    "scalar": {
        "start": "2 2 2 2 5 5 7 7 18 1 1 5 12 3 3 3 7 3 2 1 2 2 2 4 6 2 5 3 4 4 6 3 12 5 15",
        "loop": (
            "3 2 2 2 2 2 1 2 4 11 3 1 2 1 1 2 5 3 4 4 3 2 3 1 1 2 2 1 1 2 2 1 1 2 2 1 1 2 2 1 1 3 2 3 4 8 11 2 2 "
            "2 2 1 1 4 5 11 4 2 2 2 2 6 6 1 3 2 3 3 3 1 1 2 2 1 1 2 2 1 1 2 2 1 1 3 2 3 3 8 10 2 5 2 4 1 3 5 7 4 "
            "2 2 15 9 10 14 1 6 16 18 3 4 5 10 3 2 1 2 3 13 12 6 6 4 4 1 3 1 7 15 2 3 2 5 13 3 4 4 6 4 3 2 3 3 1 "
            "1 2 2 1 1 2 2 1 1 2 2 1 1 3 3 3 3 5 5"
        ),
        "end": (
            "3 2 2 2 2 2 1 2 4 11 2 1 1 1 2 1 1 1 5 7 1 2 2 3 1 4 3 2 3 3 3 4 3 3 1 8 9 2 3 2 11 16 4 4 1 6 5 7 2 "
            "5 2 3 2 4 2 11 9 2 3 2 3 1 3 5 3 2 3 2 3 2 3 2 3 6 1 6 2 3 1 1 2 2 1 3 2 1 1 2 2 3 1 1 3 3 3 2 7 12 "
            "2 4 2 10 20 24 24 24 3 3 1 1"
        ),
    },
    "vector": {
        "start": "2 2 3 3 6 1 1 4 7 1 2 1 1 1 4 1 2 1 3 5 6 1 3 1 7 3 7 6 3 1 3 2 2 1 1 5 6 1 9 6 6 7 19 1 8",
        "loop": (
            "3 2 3 3 3 6 1 3 2 9 8 3 7 4 3 2 3 3 3 3 3 3 3 2 3 5 2 7 12 2 1 2 1 3 5 3 3 3 1 2 1 1 2 3 3 9 5 6 6 3 "
            "6 3 3 3 3 3 3 2 3 5 3 7 9 1 3 3 1 3 9 3 7 4 1 3 5 2 3 3 4 6 5 3 10 3 5 21 2 3 3 3 2 1 1 2 2 1 1 2 2 "
            "1 2 3 1 7 5 1 3 5 5 3 4 1 2 3 3 5 3 3 3 6 3 1 4 5 7 1 1 5 2 1 3 6 2 2 1 4 3 1 3 4 9 5 4 1 2 3 3 2 3 "
            "3 3 3 3 3 2 2 1 1 4 4 7 7 1 1"
        ),
        "end": (
            "3 2 3 3 3 6 1 3 2 9 6 4 2 2 7 12 6 2 1 1 2 4 3 7 4 1 4 3 2 3 10 3 1 3 3 6 3 9 3 9 1 3 3 1 3 8 2 11 9 "
            "1 3 6 6 3 3 1 3 6 6 2 3 3 3 6 3 9 3 3 3 6 3 3 4 3 7 9 1 3 2 3 3 11 3 1 3 2 3 3 8 3 3 3 3 10 1 2 2 1 "
            "1 1 1 3 8 4 1 2 1 1 1 2 1 1 1 2 1 1 1 2 1 1 3 8 2 2"
        ),
    },
    "gpsimd": {
        "start": "26 26 37 15 19 6 3 8 26",
        "loop": (
            "12 27 19 6 3 3 3 3 3 3 3 3 3 3 3 20 31 19 8 3 3 3 3 3 3 3 3 3 3 3 3 3 3 28 41 11 50 59 3 50 56 3 3 3 "
            "3 3 3 3 3 3 3 3 3 3 8 8"
        ),
        "end": "12 27 9 3 10 12 3 3 3 3 3 20 40 68 32 11 6 6 3 3 3 6 3 3 3 3 62 80",
    },
}


def adaln_program(nc, a, out, n_batch):
    ctx = ExitStack()
    with ctx:
        build(nc, ctx, a, out, n_batch)


def build(nc, ctx, a, out, n_batch):
    def sb(name, shape, dt=F32):
        return ctx.enter_context(nc.sbuf_tensor(name, shape, dt))

    def per_lane(name, shape, dt=F32):
        return [sb(f"{name}_{L}", shape, dt) for L in range(LANES)]

    def sem(name):
        return ctx.enter_context(nc.semaphore(name))

    def lane_sem(name):
        return [sem(f"{name}_{L}") for L in range(LANES)]

    place, per_batch = count_uses(turnover_uses() + bank_uses())
    for name in (name for phase in FP4_PART for name in TURNOVER_USES.get(phase, [])):
        place[name] = (place[name][0], place[name][1] + per_batch[place[name][0]])
    loops = n_batch // LANES

    ident = sb("ident", [P, P])
    ident_bf = sb("ident_bf", [P, P], BF16)
    mean_w = sb("mean_w", [P, P])
    mask_bf = sb("mask_bf", [P, 2, 3 * P], BF16)
    pe_q = sb("pe_q", [P, T])
    pe_k = sb("pe_k", [P, T])
    wqkv_a = sb("wqkv_a", [P, 3 * INNER])
    wo_a = sb("wo_a", [P, CHUNKS, P])
    wqkv_b = sb("wqkv_b", [P, DEPTH, 3 * INNER])
    wo_b = sb("wo_b", [P, DEPTH, CHUNKS, P])
    w1 = sb("w1", [P, DEPTH, 2 * HID])
    w2 = sb("w2", [P, DEPTH, 3, P])
    xpos = sb("xpos", [P, DEPTH, NT, 4, DH])
    head_scale = sb("head_scale", [P, DEPTH, 4, DH])
    ln_g = sb("ln_g", [P, DEPTH])
    ln_b = sb("ln_b", [P, DEPTH])
    b1a = sb("b1a", [P, DEPTH, 3])
    b1g = sb("b1g", [P, DEPTH, 3])
    b2 = sb("b2", [P, DEPTH])
    w_c = sb("w_c", [P, 6, P])
    rope_c = sb("rope_c", [P, 4, T])
    head_rows = sb("head_rows", [P, CHEADS])
    wg_q = sb("wg_q", [P, FF])
    wu_q = sb("wu_q", [P, FF])
    wd_q = sb("wd_q", [P, 3, P])
    mod_t = sb("mod_t", [P, n_batch, 2 * N_MOD])
    c_t = sb("c_t", [P, 2, n_batch])
    eps_col = sb("eps_col", [P, 1])
    ss_bias = sb("ss_bias", [P, 1])

    x_in = per_lane("x_in", [P, NT, P])
    x_out = per_lane("x_out", [P, NT, P])
    mod = per_lane("mod", [P, 2 * N_MOD])
    xT = per_lane("xT", [P, T])
    gate_d = per_lane("gate_d", [P, 1])
    yT = per_lane("yT", [P, T])
    xT_c = yT
    shifted = per_lane("shifted", [P, T + 1])
    centred = per_lane("centred", [P, T])
    square = per_lane("square", [P, T])
    rstd = per_lane("rstd", [P, T])
    hT = per_lane("hT", [P, T])
    qT = per_lane("qT", [P, CHUNKS, T])
    kT = per_lane("kT", [P, CHUNKS, 2, T])
    v_ab = per_lane("v_ab", [P, NT, HEADS, DH])
    v_c = per_lane("v_c", [P, NT, CHEADS // 4, 4 * (CPAD + CDH)])
    negmax = per_lane("negmax", [P, 2, NT])
    probs = per_lane("probs", [P, 3, 2 * T])
    probsT = per_lane("probsT", [P, 2, 2 * T])
    z = per_lane("z", [P, 3, NT])
    rz = per_lane("rz", [P, 3, NT])
    qk_cos = per_lane("qk_cos", [P, 4, INNER])
    qk_sin = per_lane("qk_sin", [P, 2, INNER])
    oT = [t[:].rearrange("p a (c t) -> p (a c) t", t=T) for t in qk_sin]
    qk_ss = per_lane("qk_ss", [P, 4, HEADS])
    qk_rn = per_lane("qk_rn", [P, 4, HEADS])
    k_heads = per_lane("k_heads", [P, CHEADS, T])
    q_c = per_lane("q_c", [P, 2, T])
    k_c = per_lane("k_c", [P, 2, T])
    ff_h = per_lane("ff_h", [P, NT * FF])
    ff_s = per_lane("ff_s", [P, 2, NT * FF // BLOCK])

    def beside_heads(first, n):
        return [k_heads[L][:].rearrange("p a n -> p (a n)")[:, first:first + n] for L in range(LANES)]

    def thirds(views):
        return [t.rearrange("p (c t) -> p c t", c=3) for t in views]

    gelu = thirds(beside_heads(0, 3 * T))
    hid = thirds(beside_heads(3 * T, 3 * T))
    qk_sq = [t.rearrange("p (a n) -> p a n", a=2) for t in beside_heads(6 * T, 2 * INNER)]
    ff_n, ff_a, ff_c, ff_d = (beside_heads(n * NT * FF, NT * FF) for n in range(4))
    hT_q = thirds(beside_heads(4 * NT * FF, 3 * T))

    bank = [[ctx.enter_context(nc.psum_tensor(f"bank{L}_{b}", [P, 512], F32)) for b in range(4)]
            for L in range(LANES)]

    loaded = sem("loaded")
    ready_dve = sem("ready_dve")
    ready_act = sem("ready_act")
    ready_pool = sem("ready_pool")
    ready_pe = sem("ready_pe")
    x_loaded = lane_sem("x_loaded")
    x_stored = lane_sem("x_stored")
    out_ready = lane_sem("out_ready")
    mod_ready = lane_sem("mod_ready")
    filled = [[sem(f"filled{b}_{L}") for b in range(4)] for L in range(LANES)]
    taken = [[sem(f"taken{b}_{L}") for b in range(4)] for L in range(LANES)]
    s_centred = lane_sem("s_centred")
    s_square = lane_sem("s_square")
    s_logvar = lane_sem("s_logvar")
    s_rstd = lane_sem("s_rstd")
    s_newton = lane_sem("s_newton")
    s_normed = lane_sem("s_normed")
    s_h = lane_sem("s_h")
    s_x = lane_sem("s_x")
    s_xc = lane_sem("s_xc")
    s_y = lane_sem("s_y")
    s_shift = lane_sem("s_shift")
    s_max = lane_sem("s_max")
    s_rz = lane_sem("s_rz")
    s_probs = lane_sem("s_probs")
    s_o = lane_sem("s_o")
    s_qksq = lane_sem("s_qksq")
    s_qkcs = lane_sem("s_qkcs")
    s_ss = lane_sem("s_ss")
    s_ssclamp = lane_sem("s_ssclamp")
    s_logss = lane_sem("s_logss")
    s_rnorm0 = lane_sem("s_rnorm0")
    s_rnorm_step = lane_sem("s_rnorm_step")
    s_rnorm = lane_sem("s_rnorm")
    s_rotsum = lane_sem("s_rotsum")
    s_rot = lane_sem("s_rot")
    s_rot2 = lane_sem("s_rot2")
    s_hid = lane_sem("s_hid")
    s_ropec = lane_sem("s_ropec")
    s_qkc = lane_sem("s_qkc")
    s_kheads = lane_sem("s_kheads")
    s_q4 = lane_sem("s_q4")

    def is_filled(L, i, name):
        b, n = place[name]
        return filled[L][b], i * per_batch[b] + n + 1

    def is_taken(L, i, name):
        b, n = place[name]
        return taken[L][b], i * per_batch[b] + n + 2

    def is_free(L, i, name):
        b, n = place[name]
        return taken[L][b], i * per_batch[b] + n + 1

    def ps(L, name):
        return bank[L][place[name][0]]

    def sem_filled(L, name):
        return filled[L][place[name][0]]

    def sem_taken(L, name):
        return taken[L][place[name][0]]

    CORES = {"A": (0, HEADS), "B0": (HEADS, HEADS), "B1": (2 * HEADS, HEADS), "C": (3 * HEADS, CHEADS)}
    N_MAX = 2 * 3 * HEADS + CHEADS
    N_O = 3 * HEADS // GROUP + 1

    def maxima(g):
        return 2 * min(g + 1, 3 * HEADS) + max(0, g + 1 - 3 * HEADS)

    def fp4_step(dve, k, src, dst, L, step_sem, base, n):
        v = nc.vector
        nb = n // BLOCK

        def blocks(t):
            return t.rearrange("p (b e) -> p b e", e=BLOCK)

        xn, ab, hi, lo = (t[L][:, 0:n] for t in (ff_n, ff_a, ff_c, ff_d))
        scale, inv = ff_s[L][:, 0, 0:nb], ff_s[L][:, 1, 0:nb]

        def over_block(t):
            return t.unsqueeze(2).broadcast_to([P, nb, BLOCK])

        if k:
            dve.wait_ge(step_sem, base + k)
        if k == 0:
            v.tensor_reduce(inv, blocks(src), AX_X, ALU.max, apply_absolute_value=True).then_inc(step_sem, 1)
        elif k == 1:
            v.tensor_scalar(scale, inv, 1.0 / 6.0, 1e-12, ALU.mult, ALU.max).then_inc(step_sem, 1)
        elif k == 2:
            v.reciprocal(inv, scale).then_inc(step_sem, 1)
        elif k == 3:
            v.tensor_tensor(blocks(xn), blocks(src), over_block(inv), ALU.mult).then_inc(step_sem, 1)
        elif k == 4:
            v.tensor_scalar(ab.bitcast(U32), xn.bitcast(U32), 0x7FFFFFFF, None, ALU.bitwise_and).then_inc(step_sem, 1)
        elif k == 5:
            v.tensor_scalar(hi, ab, 5.0, 2.0, ALU.is_gt, ALU.mult).then_inc(step_sem, 1)
        elif k == 6:
            v.tensor_scalar(lo, ab, 1.75, None, ALU.is_gt).then_inc(step_sem, 1)
        elif k in (7, 9):
            v.scalar_tensor_tensor(hi, ab, {7: 3.5, 9: 2.5}[k], hi, ALU.is_gt, ALU.add).then_inc(step_sem, 1)
        elif k in (8, 10, 11):
            v.scalar_tensor_tensor(lo, ab, {8: 1.25, 10: 0.75, 11: 0.25}[k], lo, ALU.is_gt,
                                   ALU.add).then_inc(step_sem, 1)
        elif k == 12:
            v.scalar_tensor_tensor(hi, lo, 0.5, hi, ALU.mult, ALU.add).then_inc(step_sem, 1)
        elif k == 13:
            v.scalar_tensor_tensor(hi.bitcast(U32), xn.bitcast(U32), 0x80000000, hi.bitcast(U32),
                                   ALU.bitwise_and, ALU.bitwise_or).then_inc(step_sem, 1)
        else:
            v.tensor_tensor(blocks(dst), blocks(hi), over_block(scale), ALU.mult).then_inc(step_sem, 1)

    def setup_loads():
        yield ident[:], a["c_ident"]
        yield masks, a["c_masks"].rearrange("m p n -> p m n")
        yield pe_q[:], a["c_pe_q"]
        yield pe_k[:], a["c_pe_k"]
        yield wqkv_a[:], a["wqkv_a"]
        yield wo_a[:], a["wo_a"].rearrange("(c p) e -> p c e", p=P)
        yield wqkv_b[:], a["wqkv_b"].rearrange("l p n -> p l n")
        yield wo_b[:], a["wo_b"].rearrange("l (c p) e -> p l c e", p=P)
        yield w1[:], a["w1"].rearrange("l p n -> p l n")
        for l in range(DEPTH):
            yield w2[:, l, 0:2, :], a["w2"][l, 0:2 * P, :].rearrange("(c p) e -> p c e", p=P)
            yield w2[0:HID_ROWS[2], l, 2, :], a["w2"][l, 2 * P:HID, :]
            half = DH // 2
            for n, name in ((0, "q_scale"), (2, "k_scale")):
                row = a[name][l:l + 1, :]
                yield head_scale[:, l, n, :], row.broadcast_to([P, DH])
                yield head_scale[:, l, n + 1, 0:half], row[:, half:DH].broadcast_to([P, half])
                yield head_scale[:, l, n + 1, half:DH], row[:, 0:half].broadcast_to([P, half])
            for t, name in ((ln_g, "ln_g"), (ln_b, "ln_b"), (b2, "b2")):
                yield t[:, l:l + 1], a[name][l, :].rearrange("(p o) -> p o", o=1)
            for t, first in ((b1a, 0), (b1g, HID)):
                for c, rows in enumerate(HID_ROWS):
                    at = first + c * P
                    yield t[0:rows, l, c:c + 1], a["b1"][l, at:at + rows].rearrange("(p o) -> p o", o=1)
            yield xpos[:, l], a["c_xpos"].rearrange("t p n d -> p t n d")
        yield w_c[:], a["w_c"].rearrange("n p e -> p n e")
        yield rope_c[:], a["c_rope"].rearrange("n p t -> p n t")
        yield head_rows[:], a["c_head_rows"]
        yield c_t[:], a["c_t"].rearrange("l p b -> p l b")
        for l in range(2):
            yield w_mod[l], a["wmod"][l]
        for flat, name in ((w_nat[0], "w_gate"), (w_nat[1], "w_up")):
            yield flat[:, 0:2 * P].rearrange("p (c k) -> p c k", c=2), a[name][0:2 * P, :].rearrange("(c p) k -> p c k", p=P)
            yield flat[0:FF_ROWS[2], 2 * P:3 * P], a[name][2 * P:FF, :]
        yield ff_h[1][:, 0:FF], a["w_down"]

    masks = probs[0][:].rearrange("p t n -> p (t n)")[:, 0:2 * 3 * P].rearrange("p (m n) -> p m n", m=2)
    qk_flat = [qk_cos[l][:].rearrange("p a n -> p (a n)") for l in range(2)]
    w_mod = [t[:, 0:N_MOD * P] for t in qk_flat]
    w_nat = [t[:, N_MOD * P:(N_MOD + 3) * P] for t in qk_flat]
    n_loads = len(list(setup_loads()))
    ALL_LOADED = 16 * n_loads

    def run_program(eng, turns, core_step, phase_step):
        def run(section, steps):
            for L, i, (kind, *args) in in_turns(turns[section], [steps(L) for L in range(LANES)]):
                if kind == "core":
                    core_step(L, i, *args)
                else:
                    phase_step(L, i, kind, *args)

        run("start", start_steps)
        with eng.Fori(0, loops - 1) as i:
            run("loop", lambda L: loop_steps(L, i))
        run("end", lambda L: end_steps(L, loops - 1))

    block = ctx.enter_context(nc.Block())

    @block.sync
    def _(sp):
        sp.wait_ge(ready_pool, 1)
        for dst, src in setup_loads():
            sp.dma_start(dst, src).then_inc(loaded, 16)
        for L in range(LANES):
            sp.dma_start(x_in[L][:], a["x"][L].rearrange("(t p) e -> p t e", p=P)).then_inc(x_loaded[L], 16)
        with sp.Fori(0, loops - 1) as i:
            for L in range(LANES):
                sp.wait_ge(*is_filled(L, i, "x"))
                sp.dma_start(x_in[L][:], a["x"][bass.ds(LANES * i + LANES + L, 1)].rearrange(
                    "o (t p) e -> p (o t) e", p=P)).then_inc(x_loaded[L], 16)
            for L in range(LANES):
                sp.wait_ge(*is_taken(L, i, "out"))
                sp.dma_start(out[bass.ds(LANES * i + L, 1)].rearrange("o (t p) e -> p (o t) e", p=P),
                             x_out[L][:]).then_inc(x_stored[L], 16)
        for L in range(LANES):
            sp.wait_ge(*is_taken(L, loops - 1, "out"))
            sp.dma_start(out[n_batch - LANES + L].rearrange("(t p) e -> p t e", p=P),
                         x_out[L][:]).then_inc(x_stored[L], 16)
        for L in range(LANES):
            sp.wait_ge(x_stored[L], 16 * loops + 1)

    @block.gpsimd
    def _(pool):
        g = nc.gpsimd
        for l in range(2):
            g.memset(w_nat[l][:, 0:3 * P], 0.0)
        for L in range(LANES):
            last = g.memset(shifted[L][:, 0:1], 0.0)
        last.then_inc(ready_pool, 1)
        pool.wait_ge(ready_dve, SETUP_DVE)

        def phase_step(L, i, phase, *args):
            if phase == "x_in":
                if not (isinstance(i, int) and i == 0):
                    pool.wait_ge(s_h[L], i * N_LN)
                b = LANES * i + L
                src = mod_t[:, b, :] if isinstance(i, int) else mod_t[:, bass.ds(b, 1), :].rearrange("p o m -> p (o m)")
                g.tensor_copy(mod[L][:], src).then_inc(mod_ready[L], 1)
            elif phase == "qk":
                l, u = args
                pool.wait_ge(s_qkcs[L], i * 4 * DEPTH + 4 * l + u + 1)
                g.tensor_tensor(qk_cos[L][:, u, :], qk_cos[L][:, u, :], qk_sin[L][:, u % 2, :],
                                ALU.add).then_inc(s_rotsum[L], 1)
            elif phase == "rot":
                l, u = args
                if u in ROT_ON_VECTOR:
                    return
                pool.wait_ge(s_rnorm[L], i * DEPTH + l + 1)
                pool.wait_ge(s_rotsum[L], i * 4 * DEPTH + 4 * l + u + 1)
                r = qk_cos[L][:, u, :].rearrange("p (h d) -> p h d", d=DH)
                g.tensor_tensor(r, r, qk_rn[L][:, u, :].unsqueeze(2).broadcast_to([P, HEADS, DH]),
                                ALU.mult).then_inc(s_rot[L], 1)
            elif phase == "C.heads":
                pool.wait_ge(s_ropec[L], 2 * i + 1)
                g.tensor_tensor(k_c[L][:, 0, :], k_c[L][:, 0, :], k_c[L][:, 1, :], ALU.add).then_inc(s_qkc[L], 1)
                pool.wait_ge(s_ropec[L], 2 * i + 2)
                pool.wait_ge(s_qkc[L], 2 * i + 1)
                g.tensor_tensor(q_c[L][:, 0, :], q_c[L][:, 0, :], q_c[L][:, 1, :], ALU.add).then_inc(s_qkc[L], 1)
                for h in range(CHEADS):
                    g.tensor_scalar(k_heads[L][:, h, :], k_c[L][:, 0, :], head_rows[:, h:h + 1], 1.0,
                                    ALU.mult, ALU.mult).then_inc(s_kheads[L], 1)

        def core_step(L, i, core, part, h):
            first, heads = CORES[core]
            if part == "turn" and 1 <= h <= heads:
                head = first + h - 1
                n, end = (T, 2 * T) if core == "C" else (P, 3 * P)
                b = head % 3
                pool.wait_ge(s_rz[L], i * N_HEADS + head + 1)
                g.tensor_tensor(probs[L][:, b, 0:n], probs[L][:, b, 0:n], rz[L][:, b, 0:1].broadcast_to([P, n]),
                                ALU.mult)
                g.tensor_scalar(probs[L][:, b, n:end], probs[L][:, b, n:end], rz[L][:, b, 1:2], 1.0,
                                ALU.mult, ALU.mult).then_inc(s_probs[L], 1)

        run_program(pool, TURNS["gpsimd"], core_step, phase_step)

    @block.tensor
    def _(pe):
        mm, tp = nc.tensor.matmul, nc.tensor.transpose
        pe.wait_ge(loaded, ALL_LOADED)
        pe.wait_ge(ready_act, 1)
        for l in range(2):
            for j in range(N_MOD):
                last = mm(bank[0][l][:, j * n_batch:(j + 1) * n_batch], w_mod[l][:, j * P:(j + 1) * P],
                          c_t[:, l, :], start=True, stop=True)
        last.then_inc(ready_pe, 1)
        pe.wait_ge(ready_dve, FP4_WEIGHTS_READY)
        for l in range(2):
            for c in range(3):
                last = tp(bank[0][2 + l][:, c * P:(c + 1) * P], w_nat[l][:, c * P:(c + 1) * P], ident[:])
        for c, rows in enumerate(FF_ROWS):
            last = tp(bank[1][0][0:rows, c * P:(c + 1) * P], ff_h[1][:, c * P:c * P + rows], ident[:])
        last.then_inc(ready_pe, 1)
        pe.wait_ge(ready_dve, SETUP_DVE)
        pe.wait_ge(ready_act, SETUP_ACT)

        def scores(L, i, core, first, h):
            name = f"S{first + h}"
            s = ps(L, name)
            if h == 0:
                last_uses = {"A": ("k0", "k1", "v0", "v1"), "C": ("v",)}.get(core, ("qT0", "qT1", "kT0", "kT1"))
                for use in last_uses:
                    pe.wait_ge(*is_taken(L, i, f"{core}.{use}"))
                if core == "C":
                    pe.wait_ge(s_qkc[L], 2 * i + 2)
            pe.wait_ge(*is_free(L, i, name))
            if core == "C":
                pe.wait_ge(s_kheads[L], i * CHEADS + h + 1)
                for t in range(NT):
                    last = mm(s[:, t * T:(t + 1) * T], q_c[L][:, 0, t * P:(t + 1) * P], k_heads[L][:, h, :],
                              start=True, stop=True)
            else:
                c = h // 2
                for t, cols in ((0, slice(0, P)), (1, slice(P, 3 * P))):
                    mm(s[:, cols], ident_bf[:], mask_bf[:, 0 if core == "A" else 1, cols], start=True, stop=False)
                    last = mm(s[:, cols], qT[L][:, c, t * P:(t + 1) * P], kT[L][:, c, h % 2, 0:(t + 1) * P],
                              start=False, stop=True)
            last.then_inc(sem_filled(L, name), 1)

        def blocks_of(core):
            return [0, T, P, T + P] if core == "C" else [0, P, 2 * P]

        def turn_probs(L, i, core, g):
            pe.wait_ge(*is_free(L, i, f"P{g}"))
            pe.wait_ge(s_probs[L], i * N_HEADS + g + 1)
            for n, col in enumerate(blocks_of(core)):
                last = tp(ps(L, f"P{g}")[:, n * P:(n + 1) * P], probs[L][:, g % 3, col:col + P], ident[:])
            last.then_inc(sem_filled(L, f"P{g}"), 1)

        def weighted_values(L, i, core, first, h):
            g = first + h
            group = CHEADS if core == "C" else GROUP
            name = f"O{first + h - h % group}"
            if h % group == 0:
                pe.wait_ge(*is_free(L, i, name))
            pe.wait_ge(*is_taken(L, i, f"P{g}"))
            pt, acc = probsT[L][:, g % 2, :], ps(L, name)
            if core == "C":
                rows = slice(CPAD * (h // 4), CPAD * (h // 4 + 1))
                for s in range(NT):
                    last = mm(acc[rows, 0:T], v_c[L][:, s, h // 4, CPAD * (h % 4):CPAD * (h % 4 + 1)],
                              pt[:, s * T:(s + 1) * T], start=(h % 4 == 0 and s == 0),
                              stop=(h % 4 == 3 and s == NT - 1), tile_position=(0, CPAD * (h // 4)))
            else:
                rows, col = slice(DH * (h % 2), DH * (h % 2 + 1)), T * (h % GROUP // 2)
                mm(acc[rows, col:col + T], v_ab[L][:, 0, h, :], pt[:, 0:T], start=True, stop=False,
                   skip_group_check=True)
                last = mm(acc[rows, col + P:col + T], v_ab[L][:, 1, h, :], pt[:, T:T + P], start=False, stop=True,
                          skip_group_check=True)
            if h % group == group - 1:
                last.then_inc(sem_filled(L, name), 1)

        def core_step(L, i, core, part, h):
            first, heads = CORES[core]
            if part == "scores" and h < heads:
                scores(L, i, core, first, h)
            elif part == "turn" and 2 <= h <= heads + 1:
                turn_probs(L, i, core, first + h - 2)
            elif part == "values" and h >= 3:
                weighted_values(L, i, core, first, h - 3)

        def turned(L, i, name, pieces):
            pe.wait_ge(*is_free(L, i, name))
            for rows, col, src in pieces:
                last = tp(ps(L, name)[0:rows, col:col + P], src, ident[:])
            last.then_inc(sem_filled(L, name), 1)

        def tokens_by_features(L, i, name, src, t, w):
            pe.wait_ge(*is_free(L, i, name))
            mm(ps(L, name)[:, 0:w.shape[-1]], src[:, t * P:(t + 1) * P], w, start=True, stop=True).then_inc(
                sem_filled(L, name), 1)

        def features_by_tokens(L, i, name, products):
            pe.wait_ge(*is_free(L, i, name))
            for col, w, src in products:
                last = mm(ps(L, name)[0:w.shape[-1], col:col + T], w, src, start=True, stop=True)
            last.then_inc(sem_filled(L, name), 1)

        def phase_step(L, i, phase, *args):
            if phase == "x_in":
                pe.wait_ge(x_loaded[L], 16 * i + 16)
                turned(L, i, "x", [(P, t * P, x_in[L][:, t, :]) for t in range(NT)])
            elif phase == "mean":
                k, = args
                n_x = {0: 1, 1: 2, 4: 3}
                if k in n_x:
                    pe.wait_ge(s_x[L], 3 * i + n_x[k])
                    src = xT[L][:]
                elif k == 5:
                    pe.wait_ge(s_xc[L], 2 * i + 1)
                    src = xT_c[L][:]
                else:
                    pe.wait_ge(s_shift[L], 4 * i + 2 * (k - 2) + 2)
                    src = shifted[L][:, 0:T]
                features_by_tokens(L, i, f"mean{k}", [(0, mean_w[:], src)])
            elif phase == "var":
                k, = args
                pe.wait_ge(s_square[L], i * N_LN + k + 1)
                features_by_tokens(L, i, f"var{k}", [(0, mean_w[:], square[L][:])])
            elif phase == "A.qk":
                n, = args
                if n == 0:
                    pe.wait_ge(s_h[L], N_LN * i + 1)
                features_by_tokens(L, i, ("A.q0", "A.q1", "A.k0", "A.k1")[n],
                                   [(c * T, wqkv_a[:, (2 * n + c) * P:(2 * n + c + 1) * P], hT[L][:]) for c in range(2)])
            elif phase == "v":
                tag, t = args
                src, w = (hT[L], wqkv_a[:]) if tag == "A" else (shifted[L], wqkv_b[:, int(tag[1])])
                tokens_by_features(L, i, f"{tag}.v{t}", src, t, w[:, 2 * INNER:3 * INNER])
            elif phase == "qk":
                l, u = args
                if u == 0:
                    pe.wait_ge(s_shift[L], 4 * i + 2 * l + 1)
                which, t = u // 2, u % 2
                tokens_by_features(L, i, f"B{l}." + ("q0", "q1", "k0", "k1")[u], shifted[L], t,
                                   wqkv_b[:, l, which * INNER:(which + 1) * INNER])
            elif phase == "turn":
                l, u = args
                done = s_rot2 if u in ROT_ON_VECTOR else s_rot
                pe.wait_ge(done[L], i * 2 * DEPTH + 2 * l + u // 2 + 1)
                names = [f"B{l}.{n}" for n in ("qT0", "qT1", "kT0", "kT1")]
                turned(L, i, names[u], [(P, c * P, qk_cos[L][:, u, c * P:(c + 1) * P]) for c in range(CHUNKS)])
            elif phase == "out":
                tag, = args
                w = wo_a[:] if tag == "A" else wo_b[:, int(tag[1])]
                pe.wait_ge(*is_free(L, i, f"{tag}.out"))
                pe.wait_ge(s_o[L], i * N_O + {"A": 1, "B0": 2, "B1": 3}[tag] * (HEADS // GROUP))
                for c in range(CHUNKS):
                    last = mm(ps(L, f"{tag}.out")[:, 0:T], w[:, c, :], oT[L][:, c, :], start=(c == 0),
                              stop=(c == CHUNKS - 1))
                last.then_inc(sem_filled(L, f"{tag}.out"), 1)
            elif phase in ("gate", "up"):
                l, = args
                first, names = (HID, ("g01", "g2")) if phase == "gate" else (0, ("a01", "a2"))
                if phase == "gate":
                    pe.wait_ge(s_h[L], N_LN * i + 3 + l)
                for name, cs in zip(names, ((0, 1), (2,))):
                    features_by_tokens(L, i, f"B{l}.{name}", [
                        (n * T, w1[:, l, first + c * P:first + c * P + HID_ROWS[c]], hT[L][:]) for n, c in enumerate(cs)])
            elif phase == "down":
                l, = args
                pe.wait_ge(*is_free(L, i, f"B{l}.y"))
                for c, rows in enumerate(HID_ROWS):
                    pe.wait_ge(s_hid[L], i * 3 * DEPTH + 3 * l + c + 1)
                    last = mm(ps(L, f"B{l}.y")[:, 0:T], w2[0:rows, l, c, :], hid[L][0:rows, c, :],
                              start=(c == 0), stop=(c == 2))
                last.then_inc(sem_filled(L, f"B{l}.y"), 1)
            elif phase == "C.qk":
                pe.wait_ge(s_h[L], N_LN * i + 5)
                for name, n in (("C.k", 2), ("C.q", 0)):
                    features_by_tokens(L, i, name, [(r * T, w_c[:, n + r, :], hT[L][:]) for r in range(2)])
            elif phase == "C.v":
                pe.wait_ge(*is_free(L, i, "C.v"))
                for t in range(NT):
                    last = mm(ps(L, "C.v")[:, t * P:(t + 1) * P], hT[L][:, t * P:(t + 1) * P], w_c[:, 4, :],
                              start=True, stop=True)
                last.then_inc(sem_filled(L, "C.v"), 1)
            elif phase == "C.out":
                pe.wait_ge(s_o[L], N_O * (i + 1))
                features_by_tokens(L, i, "C.out", [(0, w_c[:, 5, :], oT[L][:, 0, :])])
            elif phase == "D.h":
                pe.wait_ge(s_h[L], N_LN * i + 6)
                turned(L, i, "D.h", [(P, t * P, hT[L][:, t * P:(t + 1) * P]) for t in range(NT)])
            elif phase == "D.xT":
                pe.wait_ge(s_q4[L], 2 * QSTEPS * i + QSTEPS)
                turned(L, i, "D.xT", [(P, t * P, ff_h[L][:, t * P:(t + 1) * P]) for t in range(NT)])
            elif phase in ("D.gate", "D.up"):
                if phase == "D.gate":
                    pe.wait_ge(*is_taken(L, i, "D.xT"))
                for t in range(NT):
                    name, w = (f"D.g{t}", wg_q) if phase == "D.gate" else (f"D.u{t}", wu_q)
                    tokens_by_features(L, i, name, oT[L][:, 0, :], t, w[:])
            elif phase == "D.hT":
                t, = args
                if t == 0:
                    pe.wait_ge(s_q4[L], 2 * QSTEPS * i + 2 * QSTEPS)
                turned(L, i, f"D.hT{t}", [(rows, c * P, ff_h[L][:, t * FF + c * P:t * FF + c * P + rows])
                                          for c, rows in enumerate(FF_ROWS)])
            elif phase == "D.out":
                pe.wait_ge(*is_free(L, i, "D.out"))
                for t in range(NT):
                    pe.wait_ge(*is_taken(L, i, f"D.hT{t}"))
                for c, rows in enumerate(FF_ROWS):
                    last = mm(ps(L, "D.out")[:, 0:T], wd_q[0:rows, c, :], hT_q[L][0:rows, c, :],
                              start=(c == 0), stop=(c == 2))
                last.then_inc(sem_filled(L, "D.out"), 1)
            elif phase == "x_out":
                pe.wait_ge(s_xc[L], 2 * i + 2)
                turned(L, i, "out", [(P, t * P, xT_c[L][:, t * P:(t + 1) * P]) for t in range(NT)])

        run_program(pe, TURNS["tensor"], core_step, phase_step)

    @block.scalar
    def _(act):
        f = nc.scalar.activation
        act.wait_ge(loaded, ALL_LOADED)
        f(c_t[:], c_t[:], ACT.Silu).then_inc(ready_act, 1)
        f(wqkv_a[:, 0:INNER], wqkv_a[:, 0:INNER], ACT.Copy, scale=DH ** -0.5).then_inc(ready_act, 1)
        act.wait_ge(ready_dve, SETUP_DVE)

        def exp_and_log_tables():
            nc.scalar.add_instruction(mybir.InstLoadActFuncSet(
                name=nc.get_next_instruction_name(), act_func_set_id=EXP_LN_SET, engine=mybir.EngineType.Activation))

        def exps(L, i, core, g):
            name = f"S{g}"
            act.wait_ge(s_max[L], i * N_MAX + maxima(g))
            ends = (T, 2 * T) if core == "C" else (P, 3 * P)
            start = 0
            for t in range(NT):
                last = f(probs[L][:, g % 3, start:ends[t]], ps(L, name)[:, start:ends[t]], ACT.Exp,
                         bias=negmax[L][:, g % 2, t:t + 1], accum_out=z[L][:, g % 3, t:t + 1])
                start = ends[t]
            last.then_inc(sem_taken(L, name), 1)

        def core_step(L, i, core, part, h):
            first, heads = CORES[core]
            if part == "scores" and h < heads:
                exps(L, i, core, first + h)
            elif part == "turn" and 2 <= h <= heads + 1:
                g = first + h - 2
                n = 2 * T if core == "C" else 3 * P
                take(L, i, f"P{g}", probsT[L][:, g % 2, 0:n], ps(L, f"P{g}")[:, 0:n])

        def take(L, i, name, dst, src, func=ACT.Copy):
            act.wait_ge(*is_filled(L, i, name))
            f(dst, src, func).then_inc(sem_taken(L, name), 1)

        def mod_col(L, n):
            return mod[L][:, n:n + 1]

        def phase_step(L, i, phase, *args):
            if phase == "centre":
                k, = args
                act.wait_ge(s_centred[L], i * N_LN + k + 1)
                f(square[L][:], centred[L][:], ACT.Square).then_inc(s_square[L], 1)
            elif phase == "rstd":
                k, = args
                act.wait_ge(*is_filled(L, i, f"var{k}"))
                f(rstd[L][:], ps(L, f"var{k}")[:, 0:T], ACT.Ln, bias=eps_col[:]).then_inc(s_logvar[L], 1)
                act.wait_ge(s_logvar[L], i * N_LN + k + 1)
                f(rstd[L][:], rstd[L][:], ACT.Exp, scale=-0.5).then_inc(s_rstd[L], 1)
            elif phase == "norm_out":
                k, = args
                gain, bias, dst = {
                    0: (mod_col(L, 1), mod_col(L, 0), hT[L]), 1: (mod_col(L, 4), mod_col(L, 3), yT[L]),
                    2: (ln_g[:, 0:1], ln_b[:, 0:1], hT[L]), 3: (ln_g[:, 1:2], ln_b[:, 1:2], hT[L]),
                    4: (mod_col(L, N_MOD + 1), mod_col(L, N_MOD), hT[L]),
                    5: (mod_col(L, N_MOD + 4), mod_col(L, N_MOD + 3), hT[L])}[k]
                if k == 0:
                    act.wait_ge(mod_ready[L], i + 1)
                act.wait_ge(s_normed[L], i * N_LN + k + 1)
                f(dst[:], centred[L][:], ACT.Identity, bias=bias, scale=gain).then_inc(s_h[L], 1)
            elif phase == "v":
                tag, t = args
                name = f"{tag}.v{t}"
                take(L, i, name, v_ab[L][:, t, :, 0:DH], ps(L, name)[:].rearrange("p (h d) -> p h d", d=DH))
            elif phase == "qk":
                l, u = args
                n = i * 4 * DEPTH + 4 * l + u
                name = f"B{l}." + ("q0", "q1", "k0", "k1")[u]
                act.wait_ge(*is_filled(L, i, name))
                if u >= 2:
                    act.wait_ge(s_ss[L], n - 1)
                f(qk_sq[L][:, u % 2, :], ps(L, name)[:], ACT.Square).then_inc(s_qksq[L], 1)
            elif phase == "rnorm":
                l, = args
                act.wait_ge(s_ssclamp[L], i * DEPTH + l + 1)
                f(qk_rn[L][:], qk_ss[L][:], ACT.Ln, scale=SS_SCALE).then_inc(s_logss[L], 1)
                act.wait_ge(s_logss[L], i * DEPTH + l + 1)
                f(qk_rn[L][:], qk_rn[L][:], ACT.Exp, scale=-0.5, bias=ss_bias[:]).then_inc(s_rnorm0[L], 1)
            elif phase == "turn":
                l, u = args
                name = f"B{l}." + ("qT0", "qT1", "kT0", "kT1")[u]
                cols = slice((u % 2) * P, (u % 2 + 1) * P)
                src = ps(L, name)[:].rearrange("p (c n) -> p c n", c=CHUNKS)
                if u < 2:
                    take(L, i, name, qT[L][:, :, cols], src)
                else:
                    act.wait_ge(*is_filled(L, i, name))
                    for half in range(2):
                        rows = slice(DH * half, DH * (half + 1))
                        last = f(kT[L][rows, :, half, cols], src[rows], ACT.Copy)
                    last.then_inc(sem_taken(L, name), 1)
            elif phase == "gate":
                l, = args
                for name, cs in (("g01", (0, 1)), ("g2", (2,))):
                    act.wait_ge(*is_filled(L, i, f"B{l}.{name}"))
                    for n, c in enumerate(cs):
                        rows = HID_ROWS[c]
                        last = f(gelu[L][0:rows, c, :], ps(L, f"B{l}.{name}")[0:rows, n * T:(n + 1) * T], ACT.Gelu,
                                 bias=b1g[0:rows, l, c:c + 1])
                    last.then_inc(sem_taken(L, f"B{l}.{name}"), 1)
                exp_and_log_tables()
            elif phase == "C.v":
                take(L, i, "C.v", v_c[L][:].rearrange("p t g (j n) -> p (t g) j n", j=4)[:, :, :, 0:CDH],
                     ps(L, "C.v")[:, 0:T].rearrange("p (g j d) -> p g j d", j=4, d=CDH))
            elif phase == "D.xT":
                take(L, i, "D.xT", oT[L][:, 0, :], ps(L, "D.xT")[:, 0:T])
            elif phase == "D.gate":
                for t in range(NT):
                    take(L, i, f"D.g{t}", ff_a[L][:, t * FF:(t + 1) * FF], ps(L, f"D.g{t}")[:, 0:FF], ACT.Silu)
                exp_and_log_tables()
            elif phase == "D.hT":
                t, = args
                act.wait_ge(*is_filled(L, i, f"D.hT{t}"))
                for c, rows in enumerate(FF_ROWS):
                    last = f(hT_q[L][0:rows, c, t * P:(t + 1) * P], ps(L, f"D.hT{t}")[0:rows, c * P:(c + 1) * P], ACT.Copy)
                last.then_inc(sem_taken(L, f"D.hT{t}"), 1)
            elif phase == "x_out":
                act.wait_ge(x_stored[L], 16 * i + 1)
                take(L, i, "out", x_out[L][:], ps(L, "out")[:, 0:T].rearrange("p (t e) -> p t e", t=NT))

        exp_and_log_tables()
        run_program(act, TURNS["scalar"], core_step, phase_step)

    @block.vector
    def _(dve):
        v = nc.vector
        v.memset(mean_w[:], 1.0 / P)
        v.memset(eps_col[:], 1e-5)
        v.memset(ss_bias[:], 0.5 * math.log(SS_SCALE))
        for L in range(LANES):
            for b in range(4):
                v.engine_nop().then_inc(taken[L][b], 1)
            v.engine_nop().then_inc(x_stored[L], 1)
            v.memset(v_c[L][:], 0.0)
            v.memset(kT[L][:], 0.0)
        dve.wait_ge(loaded, ALL_LOADED)
        v.tensor_copy(ident_bf[:], ident[:])
        v.tensor_copy(mask_bf[:], masks)
        for l in range(DEPTH):
            for t in range(NT):
                v.tensor_tensor(xpos[:, l, t], xpos[:, l, t], head_scale[:, l], ALU.mult)
        dve.wait_ge(ready_pe, 1)
        for l in range(2):
            m = bank[0][l][:, 0:N_MOD * n_batch].rearrange("p (j b) -> p b j", j=N_MOD)
            out_m = mod_t[:, :, l * N_MOD:(l + 1) * N_MOD]
            last = v.tensor_copy(out_m, m)
        last.then_inc(ready_dve, 1)
        dve.wait_ge(ready_dve, 1)
        gates = mod_t[:].rearrange("p b (g j) -> p b g j", j=3)
        sign = qk_sin[0][:, 0, 0:4 * n_batch].rearrange("p (b g) -> p b g", g=4)
        size = qk_sin[0][:, 1, 0:4 * n_batch].rearrange("p (b g) -> p b g", g=4)
        v.tensor_scalar(gates[:, :, :, 1], gates[:, :, :, 1], 1.0, None, ALU.add)
        v.tensor_scalar(sign, gates[:, :, :, 2], 0.0, 2.0, ALU.is_ge, ALU.mult)
        v.tensor_copy(size, gates[:, :, :, 2]).then_inc(ready_dve, 1)
        dve.wait_ge(ready_dve, 2)
        v.scalar_tensor_tensor(size, size, -1.0, size, ALU.mult, ALU.max).then_inc(ready_dve, 1)
        dve.wait_ge(ready_dve, 3)
        v.tensor_scalar(size, size, 0.25, None, ALU.max).then_inc(ready_dve, 1)
        dve.wait_ge(ready_dve, 4)
        v.scalar_tensor_tensor(sign, sign, -1.0, size, ALU.add, ALU.mult).then_inc(ready_dve, 1)
        dve.wait_ge(ready_dve, 5)
        v.tensor_copy(gates[:, :, :, 2], sign).then_inc(ready_dve, 1)
        for n, (w, cols) in enumerate(((w_nat[0], 3 * P), (w_nat[1], 3 * P), (ff_h[1], FF))):
            base = MOD_READY + n * QSTEPS
            dve.wait_ge(ready_dve, base)
            for k in range(QSTEPS):
                fp4_step(dve, k, w[:, 0:cols], w[:, 0:cols], 0, ready_dve, base, cols)
        dve.wait_ge(ready_pe, 2)
        v.tensor_copy(wg_q[:], bank[0][2][:, 0:FF])
        v.tensor_copy(wu_q[:], bank[0][3][:, 0:FF])
        for c, rows in enumerate(FF_ROWS):
            last = v.tensor_copy(wd_q[0:rows, c, :], bank[1][0][0:rows, c * P:(c + 1) * P])
        last.then_inc(ready_dve, 1)

        def row_max(L, i, core, g):
            name = f"S{g}"
            dve.wait_ge(*is_filled(L, i, name))
            if core == "C":
                v.tensor_reduce(negmax[L][:, g % 2, :], ps(L, name)[:].rearrange("p (t n) -> p t n", t=NT), AX_X,
                                ALU.max, negate=True).then_inc(s_max[L], 1)
            else:
                v.tensor_reduce(negmax[L][:, g % 2, 0:1], ps(L, name)[:, 0:P], AX_X, ALU.max,
                                negate=True).then_inc(s_max[L], 1)
                v.tensor_reduce(negmax[L][:, g % 2, 1:2], ps(L, name)[:, P:3 * P], AX_X, ALU.max,
                                negate=True).then_inc(s_max[L], 1)

        def sums_reciprocal(L, i, core, g):
            dve.wait_ge(*is_taken(L, i, f"S{g}"))
            v.reciprocal(rz[L][:, g % 3, :], z[L][:, g % 3, :]).then_inc(s_rz[L], 1)

        def take_outputs(L, i, core, first, h):
            if core == "C":
                name, dst, src = f"O{first}", oT[L][:, 0, :], ps(L, f"O{first}")[:, 0:T]
            else:
                name = f"O{first + h - GROUP + 1}"
                c = (h - GROUP + 1) // 2
                dst, src = oT[L][:, c:c + GROUP // 2, :], ps(L, name)[:].rearrange("p (c t) -> p c t", t=T)
            dve.wait_ge(*is_filled(L, i, name))
            v.tensor_copy(dst, src).then_inc(s_o[L], 1)
            v.engine_nop().then_inc(sem_taken(L, name), 1)

        def core_step(L, i, core, part, h):
            first, heads = CORES[core]
            group = CHEADS if core == "C" else GROUP
            if part == "scores" and h < heads:
                row_max(L, i, core, first + h)
            elif part == "turn" and 1 <= h <= heads:
                sums_reciprocal(L, i, core, first + h - 1)
            elif part == "values" and h >= 3 and (h - 3) % group == group - 1:
                take_outputs(L, i, core, first, h - 3)

        def phase_step(L, i, phase, *args):
            if phase == "no_use":
                name, = args
                n = i * per_batch[place[name][0]] + place[name][1]
                if n:
                    dve.wait_ge(sem_filled(L, name), n)
                v.engine_nop().then_inc(sem_filled(L, name), 1)
                dve.wait_ge(sem_taken(L, name), n + 1)
                v.engine_nop().then_inc(sem_taken(L, name), 1)
            elif phase == "x_in":
                dve.wait_ge(*is_filled(L, i, "x"))
                v.tensor_copy(xT[L][:], ps(L, "x")[:, 0:T]).then_inc(s_x[L], 1)
                v.engine_nop().then_inc(sem_taken(L, "x"), 1)
            elif phase == "centre":
                k, = args
                if k in (2, 3):
                    dve.wait_ge(s_shift[L], 4 * i + 2 * (k - 2) + 2)
                elif k == 5:
                    dve.wait_ge(s_xc[L], 2 * i + 1)
                else:
                    dve.wait_ge(s_x[L], 3 * i + {0: 1, 1: 2, 4: 3}[k])
                src = shifted[L][:, 0:T] if k in (2, 3) else xT_c[L][:] if k == 5 else xT[L][:]
                dve.wait_ge(*is_filled(L, i, f"mean{k}"))
                v.tensor_tensor(centred[L][:], src, ps(L, f"mean{k}")[:, 0:T], ALU.subtract).then_inc(s_centred[L], 1)
                v.engine_nop().then_inc(sem_taken(L, f"mean{k}"), 1)
            elif phase == "newton":
                k, = args
                n = 3 * (i * N_LN + k)
                dve.wait_ge(s_rstd[L], i * N_LN + k + 1)
                v.scalar_tensor_tensor(square[L][:], ps(L, f"var{k}")[:, 0:T], 1e-5, rstd[L][:], ALU.add,
                                       ALU.mult).then_inc(s_newton[L], 1)
                v.tensor_tensor(centred[L][:], centred[L][:], rstd[L][:], ALU.mult).then_inc(s_newton[L], 1)
                dve.wait_ge(s_newton[L], n + 1)
                v.scalar_tensor_tensor(square[L][:], square[L][:], -0.5, rstd[L][:], ALU.mult,
                                       ALU.mult).then_inc(s_newton[L], 1)
                v.engine_nop().then_inc(sem_taken(L, f"var{k}"), 1)
                dve.wait_ge(s_newton[L], n + 3)
                v.scalar_tensor_tensor(centred[L][:], square[L][:], 1.5, centred[L][:], ALU.add,
                                       ALU.mult).then_inc(s_normed[L], 1)
            elif phase == "A.qk":
                n, = args
                name = ("A.q0", "A.q1", "A.k0", "A.k1")[n]
                c = 2 * (n % 2)
                src = ps(L, name)[:].rearrange("p (c t) -> p c t", c=2)
                dve.wait_ge(*is_filled(L, i, name))
                if n < 2:
                    last = v.tensor_tensor(qT[L][:, c:c + 2, :], src, pe_q[:].unsqueeze(1).broadcast_to([P, 2, T]),
                                           ALU.add)
                else:
                    for half in range(2):
                        rows = slice(DH * half, DH * (half + 1))
                        last = v.tensor_tensor(kT[L][rows, c:c + 2, half, :], src[rows],
                                               pe_k[rows].unsqueeze(1).broadcast_to([DH, 2, T]), ALU.add)
                last.then_inc(sem_taken(L, name), 1)
            elif phase == "out":
                tag, = args
                name = f"{tag}.out"
                dve.wait_ge(*is_filled(L, i, name))
                if tag == "A":
                    v.scalar_tensor_tensor(xT[L][:], ps(L, name)[:, 0:T], mod[L][:, 2:3], xT[L][:],
                                           ALU.mult, ALU.add).then_inc(s_x[L], 1)
                else:
                    v.tensor_tensor(yT[L][:], ps(L, name)[:, 0:T], yT[L][:], ALU.add).then_inc(s_y[L], 1)
                v.engine_nop().then_inc(sem_taken(L, name), 1)
            elif phase == "shift":
                n, = args
                if n:
                    dve.wait_ge(s_y[L], 4 * i + n)
                else:
                    dve.wait_ge(s_h[L], i * N_LN + 2)
                v.tensor_copy(shifted[L][0:P // 2, 0:T], yT[L][0:P // 2, :])
                v.tensor_copy(shifted[L][P // 2:P, 1:T + 1], yT[L][P // 2:P, :]).then_inc(s_shift[L], 1)
            elif phase == "qk":
                l, u = args
                n = i * 4 * DEPTH + 4 * l + u
                t, which, half = u % 2, u // 2, DH // 2
                name = f"B{l}." + ("q0", "q1", "k0", "k1")[u]
                src = ps(L, name)[:].rearrange("p (h d) -> p h d", d=DH)

                def table(m, lo, hi):
                    return xpos[:, l, t, m, lo:hi].unsqueeze(1).broadcast_to([P, HEADS, hi - lo])

                cos = qk_cos[L][:, u, :].rearrange("p (h d) -> p h d", d=DH)
                sin = qk_sin[L][:, u % 2, :].rearrange("p (h d) -> p h d", d=DH)
                dve.wait_ge(s_qksq[L], n + 1)
                v.tensor_tensor(cos, src, table(2 * which, 0, DH), ALU.mult)
                if u >= 2:
                    dve.wait_ge(s_rotsum[L], n - 1)
                v.tensor_tensor(sin[:, :, 0:half], src[:, :, half:DH], table(2 * which + 1, 0, half), ALU.mult)
                v.tensor_tensor(sin[:, :, half:DH], src[:, :, 0:half], table(2 * which + 1, half, DH),
                                ALU.mult).then_inc(s_qkcs[L], 1)
                v.tensor_reduce(qk_ss[L][:, u, :], qk_sq[L][:, u % 2, :].rearrange("p (h d) -> p h d", d=DH),
                                AX_X, ALU.add).then_inc(s_ss[L], 1)
                v.engine_nop().then_inc(sem_taken(L, name), 1)
                if u == 3:
                    dve.wait_ge(s_ss[L], n + 1)
                    v.tensor_scalar(qk_ss[L][:], qk_ss[L][:], 1e-24, None, ALU.max).then_inc(s_ssclamp[L], 1)
            elif phase == "rnorm":
                l, = args
                n = 3 * (i * DEPTH + l)
                ss, y = qk_ss[L][:], qk_rn[L][:]
                dve.wait_ge(s_rnorm0[L], i * DEPTH + l + 1)
                v.tensor_tensor(ss, ss, y, ALU.mult).then_inc(s_rnorm_step[L], 1)
                dve.wait_ge(s_rnorm_step[L], n + 1)
                v.tensor_tensor(ss, ss, y, ALU.mult).then_inc(s_rnorm_step[L], 1)
                dve.wait_ge(s_rnorm_step[L], n + 2)
                v.tensor_scalar(ss, ss, -0.5, 1.5, ALU.mult, ALU.add).then_inc(s_rnorm_step[L], 1)
                dve.wait_ge(s_rnorm_step[L], n + 3)
                v.tensor_tensor(y, y, ss, ALU.mult).then_inc(s_rnorm[L], 1)
            elif phase == "rot":
                l, u = args
                if u in ROT_ON_VECTOR:
                    dve.wait_ge(s_rotsum[L], i * 4 * DEPTH + 4 * l + u + 1)
                    dve.wait_ge(s_rnorm[L], i * DEPTH + l + 1)
                    rotated = qk_cos[L][:, u, :].rearrange("p (h d) -> p h d", d=DH)
                    v.tensor_tensor(rotated, rotated, qk_rn[L][:, u, :].unsqueeze(2).broadcast_to([P, HEADS, DH]),
                                    ALU.mult).then_inc(s_rot2[L], 1)
            elif phase == "up":
                l, = args
                for name, other, cs in (("a01", "g01", (0, 1)), ("a2", "g2", (2,))):
                    dve.wait_ge(*is_filled(L, i, f"B{l}.{name}"))
                    dve.wait_ge(*is_taken(L, i, f"B{l}.{other}"))
                    for n, c in enumerate(cs):
                        rows = HID_ROWS[c]
                        v.scalar_tensor_tensor(hid[L][0:rows, c, :], ps(L, f"B{l}.{name}")[0:rows, n * T:(n + 1) * T],
                                               b1a[0:rows, l, c:c + 1], gelu[L][0:rows, c, :], ALU.add,
                                               ALU.mult).then_inc(s_hid[L], 1)
                    v.engine_nop().then_inc(sem_taken(L, f"B{l}.{name}"), 1)
            elif phase == "down":
                l, = args
                dve.wait_ge(*is_filled(L, i, f"B{l}.y"))
                v.scalar_tensor_tensor(yT[L][:], ps(L, f"B{l}.y")[:, 0:T], b2[:, l:l + 1], yT[L][:],
                                       ALU.add, ALU.add).then_inc(s_y[L], 1)
                v.engine_nop().then_inc(sem_taken(L, f"B{l}.y"), 1)
            elif phase == "x_of_B":
                v.tensor_copy(gate_d[L][:], mod[L][:, 2 * N_MOD - 1:2 * N_MOD])
                dve.wait_ge(s_y[L], 4 * i + 4)
                v.scalar_tensor_tensor(xT[L][:], yT[L][:], mod[L][:, 5:6], xT[L][:], ALU.mult,
                                       ALU.add).then_inc(s_x[L], 1)
            elif phase == "C.qk":
                for dst, name, n in ((k_c[L], "C.k", 2), (q_c[L], "C.q", 0)):
                    dve.wait_ge(*is_filled(L, i, name))
                    v.tensor_tensor(dst[:], ps(L, name)[:].rearrange("p (r t) -> p r t", r=2), rope_c[:, n:n + 2, :],
                                    ALU.mult).then_inc(s_ropec[L], 1)
                    v.engine_nop().then_inc(sem_taken(L, name), 1)
            elif phase == "C.out":
                dve.wait_ge(*is_filled(L, i, "C.out"))
                v.scalar_tensor_tensor(xT_c[L][:], ps(L, "C.out")[:, 0:T], mod[L][:, N_MOD + 2:N_MOD + 3], xT[L][:],
                                       ALU.mult, ALU.add).then_inc(s_xc[L], 1)
                v.engine_nop().then_inc(sem_taken(L, "C.out"), 1)
            elif phase == "D.quant":
                which, k = args
                if which == 0:
                    if k == 0:
                        dve.wait_ge(*is_filled(L, i, "D.h"))
                    fp4_step(dve, k, ps(L, "D.h")[:, 0:T], ff_h[L][:, 0:T], L, s_q4[L], 2 * QSTEPS * i, T)
                    if k == 3:
                        v.engine_nop().then_inc(sem_taken(L, "D.h"), 1)
                else:
                    if k == 0:
                        for t in range(NT):
                            dve.wait_ge(*is_taken(L, i, f"D.u{t}"))
                    fp4_step(dve, k, ff_h[L][:], ff_h[L][:], L, s_q4[L], (2 * i + 1) * QSTEPS, NT * FF)
            elif phase == "D.up":
                for t in range(NT):
                    dve.wait_ge(*is_filled(L, i, f"D.u{t}"))
                    dve.wait_ge(*is_taken(L, i, f"D.g{t}"))
                    v.tensor_tensor(ff_h[L][:, t * FF:(t + 1) * FF], ps(L, f"D.u{t}")[:, 0:FF],
                                    ff_a[L][:, t * FF:(t + 1) * FF], ALU.mult).then_inc(sem_taken(L, f"D.u{t}"), 1)
            elif phase == "D.out":
                dve.wait_ge(*is_filled(L, i, "D.out"))
                v.scalar_tensor_tensor(xT_c[L][:], ps(L, "D.out")[:, 0:T], gate_d[L][:], xT_c[L][:],
                                       ALU.mult, ALU.add).then_inc(s_xc[L], 1)
                v.engine_nop().then_inc(sem_taken(L, "D.out"), 1)

        run_program(dve, TURNS["vector"], core_step, phase_step)


MOD_READY = 6
FP4_WEIGHTS_READY = MOD_READY + 3 * QSTEPS
SETUP_DVE = FP4_WEIGHTS_READY + 1
SETUP_ACT = 2


def shape_constants():
    import numpy as np

    f = np.float32
    c = {}
    c["c_ident"] = np.eye(P, dtype=f)
    i, j = np.arange(P)[:, None], np.arange(P)[None, :]
    off = f(-1e30)
    zero = np.zeros((P, P), f)
    causal = np.where(j <= i, zero, off)
    band = np.where((j <= i) & (i <= j + WINDOW), zero, off)
    before = np.where(i + P <= j + WINDOW, zero, off)
    c["c_masks"] = np.stack([np.concatenate([causal, zero, causal], 1), np.concatenate([band, before, band], 1)])
    pos = np.arange(T, dtype=f)[:, None]
    div = np.exp(np.arange(0, DH, 2, dtype=f) * f(-np.log(10000.0) / DH)).astype(f)
    ang = (pos * div).astype(f)
    pe = np.stack([np.sin(ang), np.cos(ang)], -1).reshape(T, DH).astype(f)
    c["c_pe_k"] = np.concatenate([pe.T, pe.T], 0)
    c["c_pe_q"] = c["c_pe_k"] * f(DH ** -0.5)
    half = np.arange(0, DH, 2, dtype=f)
    inv_freq = (f(1.0) / f(10000.0) ** (half / f(DH))).astype(f)
    freqs = np.concatenate([pos * inv_freq[None]] * 2, -1).astype(f)
    base = ((half + f(0.4 * DH)) / f(1.4 * DH)).astype(f)
    power = ((pos[:, 0] - T // 2) / f(WINDOW // 2)).astype(f)
    decay = np.concatenate([base[None] ** power[:, None]] * 2, -1).astype(f)
    sign = np.concatenate([-np.ones(DH // 2, f), np.ones(DH // 2, f)])
    cos, sin = np.cos(freqs), np.sin(freqs) * sign
    c["c_xpos"] = np.stack([f(8) * cos * decay, f(8) * sin * decay, cos / decay, sin / decay], 1).reshape(
        NT, P, 4, DH).astype(f)
    fr = np.exp(f(-np.log(10000.0)) * np.arange(0, CDH, 2, dtype=f) / f(CDH)).astype(f)
    ang = (pos * fr).astype(f)
    cosc = np.tile(np.repeat(np.cos(ang).T, 2, 0), (CHEADS, 1))
    sinc = np.tile((np.stack([-np.sin(ang), np.sin(ang)], -1).reshape(T, CDH)).T, (CHEADS, 1))
    s = f(CDH ** -0.5)
    c["c_rope"] = np.stack([cosc * s, sinc * s, cosc, sinc]).astype(f)
    c["c_head_rows"] = (np.arange(P)[:, None] // CDH == np.arange(CHEADS)[None, :]).astype(f)
    return c


def laid_out(inputs):
    import numpy as np

    x = {k: np.asarray(v) for k, v in inputs.items()}
    w = x["L0_attn_Wqkv"].reshape(HEADS, 3, DH, P).transpose(1, 0, 2, 3).reshape(3 * INNER, P)
    swap = np.arange(P) ^ 1
    return {
        "x": x["L0_attn_x"],
        "wqkv_a": w.T,
        "wo_a": x["L0_attn_Wo"].T,
        "wqkv_b": x["L0_ffn_wqkv"], "wo_b": x["L0_ffn_wo"], "w1": x["L0_ffn_w1"], "w2": x["L0_ffn_w2"],
        "q_scale": x["L0_ffn_q_scale"], "k_scale": x["L0_ffn_k_scale"],
        "ln_g": x["L0_ffn_ln_g"], "ln_b": x["L0_ffn_ln_b"], "b1": x["L0_ffn_b1"], "b2": x["L0_ffn_b2"],
        "c_t": np.stack([x["L0_c"].T, x["L1_c"].T]),
        "wmod": np.stack([x["L0_wmod"], x["L1_wmod"]]),
        "w_c": np.stack([x["L1_attn_W_q"].T, x["L1_attn_W_q"][swap].T, x["L1_attn_W_k"].T,
                         x["L1_attn_W_k"][swap].T, x["L1_attn_W_v"].T, x["L1_attn_W_o"].T]),
        "w_gate": x["L1_ffn_w_gate"], "w_up": x["L1_ffn_w_up"], "w_down": x["L1_ffn_w_down"],
    }


def prepare(inputs, bacc):
    import numpy as np

    nc = bacc.Bacc("TRN2", target_bir_lowering=False, num_devices=1)
    nc.disable_value_cache = True
    consts = shape_constants()
    arrays, aps = {}, {}
    for name, v in {**laid_out(inputs), **consts}.items():
        v = np.ascontiguousarray(v)
        arrays[f"in_{name}"] = v
        aps[name] = nc.dram_tensor(f"in_{name}", v.shape, mybir.dt.from_np(v.dtype), kind="ExternalInput").ap()
    n_batch = aps["x"].shape[0]
    out = nc.dram_tensor("out_x", (n_batch, T, P), F32, kind="ExternalOutput").ap()
    adaln_program(nc, aps, out, n_batch)
    return nc, arrays


def kernel(**inputs):
    import concourse.bacc as bacc
    from concourse.bass_utils import run_bass_kernel_spmd

    nc, arrays = prepare(inputs, bacc)
    result = run_bass_kernel_spmd(nc, [arrays], core_ids=[0])
    return result.results[0]["out_x"]
```
